# Optimizing a Trainium2 kernel written in Bass

```python
import numpy as np
import jax
import jax.numpy as jnp

def _softmax(x, axis=-1):
    return jax.nn.softmax(x, axis=axis)

def _gelu(x):
    return jax.nn.gelu(x, approximate=True)

def _silu(x):
    return jax.nn.silu(x)

def _sigmoid(x):
    return jax.nn.sigmoid(x)

def _layernorm(x, axis=-1, eps=1e-05):
    m = jnp.mean(x, axis=axis, keepdims=True)
    v = jnp.var(x, axis=axis, keepdims=True)
    return (x - m) / jnp.sqrt(v + eps)

def _scatter_add(tgt, idx, src, axis=0):
    return tgt.at[idx].add(src)

def _segment_sum(src, seg, n):
    return jax.ops.segment_sum(src, seg, n)
kernel_name = 'mk_adaln_d1_jaxref_r8_800b0b'

def setup_inputs(seed: int=0):
    np.random.seed(seed)
    _w = jnp.asarray

    def _L0_attn_setup():
        import jax, jax.numpy as jnp
        import numpy as np
        D = 128
        H = 16
        KVH = 4
        HD = D // H
        LAT = 32
        WIN = 32
        B, S = (1, 256)
        BASE_G, BASE_L = (1000000.0, 10000.0)
        EPS = 1e-06

        def rmsnorm(x, w):
            return x * jax.lax.rsqrt(jnp.mean(x * x, axis=-1, keepdims=True) + EPS) * w

        def qk_norm(x):
            return x * jax.lax.rsqrt(jnp.mean(x * x, axis=-1, keepdims=True) + EPS)

        def rope(x, base):
            s, hd = (x.shape[-2], x.shape[-1])
            inv_freq = 1.0 / base ** (jnp.arange(0, hd, 2, dtype=jnp.float32) / hd)
            freqs = jnp.arange(s, dtype=jnp.float32)[:, None] * inv_freq[None, :]
            cos, sin = (jnp.cos(freqs), jnp.sin(freqs))
            xe, xo = (x[..., ::2], x[..., 1::2])
            out = jnp.stack([xe * cos - xo * sin, xe * sin + xo * cos], axis=-1)
            return out.reshape(x.shape)

        def split_heads(x, n_heads):
            b, s, _ = x.shape
            return x.reshape(b, s, n_heads, HD).transpose(0, 2, 1, 3)

        def repeat_kv(x):
            return jnp.repeat(x, H // KVH, axis=1)

        def sdpa(q, k, v, mask):
            scores = jnp.einsum('bhqd,bhkd->bhqk', q, k) / np.sqrt(HD).astype(np.float32)
            scores = jnp.where(mask, scores, jnp.float32(-1e+30))
            probs = jax.nn.softmax(scores, axis=-1)
            return jnp.einsum('bhqk,bhkd->bhqd', probs, v)

        def merge_heads(x):
            b, h, s, hd = x.shape
            return x.transpose(0, 2, 1, 3).reshape(b, s, h * hd)

        def global_latent_attn(x, wq, w_kv_down, w_k_up, w_v_up, wo):
            q = split_heads(x @ wq, H)
            latent = x @ w_kv_down
            k = split_heads(latent @ w_k_up, KVH)
            v = split_heads(latent @ w_v_up, KVH)
            q, k = (rope(q, BASE_G), rope(k, BASE_G))
            q, k = (qk_norm(q), qk_norm(k))
            k, v = (repeat_kv(k), repeat_kv(v))
            i = jnp.arange(x.shape[1])
            causal = i[:, None] >= i[None, :]
            return merge_heads(sdpa(q, k, v, causal)) @ wo

        def local_gqa_attn(x, wq, wk, wv, wo):
            q = split_heads(x @ wq, H)
            k = split_heads(x @ wk, KVH)
            v = split_heads(x @ wv, KVH)
            q, k = (rope(q, BASE_L), rope(k, BASE_L))
            q, k = (qk_norm(q), qk_norm(k))
            k, v = (repeat_kv(k), repeat_kv(v))
            i = jnp.arange(x.shape[1])
            diff = i[:, None] - i[None, :]
            mask = (diff >= 0) & (diff < WIN)
            return merge_heads(sdpa(q, k, v, mask)) @ wo
        key = jax.random.key(seed)
        ks = jax.random.split(key, 12)
        std = 0.02
        return {'hidden': jax.random.normal(ks[0], (B, S, D), dtype=jnp.float32), 'norm1_w': jnp.ones((D,), jnp.float32), 'norm2_w': jnp.ones((D,), jnp.float32), 'g_wq': jax.random.normal(ks[1], (D, H * HD), jnp.float32) * std, 'g_kv_down': jax.random.normal(ks[2], (D, LAT), jnp.float32) * std, 'g_k_up': jax.random.normal(ks[3], (LAT, KVH * HD), jnp.float32) * std, 'g_v_up': jax.random.normal(ks[4], (LAT, KVH * HD), jnp.float32) * std, 'g_wo': jax.random.normal(ks[5], (D, D), jnp.float32) * std, 'l_wq': jax.random.normal(ks[6], (D, H * HD), jnp.float32) * std, 'l_wk': jax.random.normal(ks[7], (D, KVH * HD), jnp.float32) * std, 'l_wv': jax.random.normal(ks[8], (D, KVH * HD), jnp.float32) * std, 'l_wo': jax.random.normal(ks[9], (D, D), jnp.float32) * std}
    _L0_attn_in = _L0_attn_setup()

    def _L0_ffn_setup():
        import jax, jax.numpy as jnp
        import numpy as np
        DIM = 128
        DEPTH = 2
        HEADS = 8
        DIM_HEAD = 64
        WINDOW = 64
        INNER = HEADS * DIM_HEAD
        HID = int(DIM * 4 * 2 / 3)
        B, N = (2, 1024)
        QK_SCALE = 8.0

        def shift_token(t):
            t1, t2 = jnp.split(t, 2, axis=-1)
            t2 = jnp.pad(t2, ((0, 0), (1, 0), (0, 0)))[:, :-1]
            return jnp.concatenate([t1, t2], axis=-1)

        def l2norm(t):
            return t / jnp.clip(jnp.linalg.norm(t, axis=-1, keepdims=True), 1e-12)

        def rotate_half(x):
            x1, x2 = jnp.split(x, 2, axis=-1)
            return jnp.concatenate([-x2, x1], axis=-1)

        def rotary_xpos(q, k):
            n = q.shape[-2]
            half_idx = jnp.arange(0, DIM_HEAD, 2, dtype=jnp.float32)
            inv_freq = 1.0 / 10000.0 ** (half_idx / DIM_HEAD)
            t = jnp.arange(n, dtype=jnp.float32)
            freqs = t[:, None] * inv_freq[None, :]
            freqs = jnp.concatenate([freqs, freqs], axis=-1)
            base = (half_idx + 0.4 * DIM_HEAD) / (1.4 * DIM_HEAD)
            power = (t - n // 2) / float(WINDOW // 2)
            scale = base[None, :] ** power[:, None]
            scale = jnp.concatenate([scale, scale], axis=-1)
            cos, sin = (jnp.cos(freqs), jnp.sin(freqs))
            q = q * cos * scale + rotate_half(q) * sin * scale
            k = k * cos / scale + rotate_half(k) * sin / scale
            return (q, k)

        def local_attention(q, k, v):
            b, h, n, d = q.shape
            w = n // WINDOW
            bq = q.reshape(b, h, w, WINDOW, d) * QK_SCALE
            bk = k.reshape(b, h, w, WINDOW, d)
            bv = v.reshape(b, h, w, WINDOW, d)

            def look_around(t):
                p = jnp.pad(t, ((0, 0), (0, 0), (1, 0), (0, 0), (0, 0)))
                return jnp.concatenate([p[:, :, :w], p[:, :, 1:]], axis=3)
            bk, bv = (look_around(bk), look_around(bv))
            bt = jnp.arange(n).reshape(w, WINDOW)
            btp = jnp.pad(bt, ((1, 0), (0, 0)), constant_values=-1)
            btk = jnp.concatenate([btp[:w], btp[1:]], axis=1)
            sim = jnp.einsum('bhwid,bhwjd->bhwij', bq, bk)
            i = bt[:, :, None]
            j = btk[:, None, :]
            mask = (i < j) | (i > j + WINDOW) | (j == -1)
            sim = jnp.where(mask, -jnp.finfo(sim.dtype).max, sim)
            attn = jax.nn.softmax(sim, axis=-1)
            out = jnp.einsum('bhwij,bhwjd->bhwid', attn, bv)
            return out.reshape(b, h, n, d)

        def _layer(x, wqkv, qs, ksc, wo, lg, lb, w1, b1, w2, b2):
            b, n, _ = x.shape
            h = shift_token(x)
            qkv = h @ wqkv
            q, k, v = jnp.split(qkv, 3, axis=-1)
            to_heads = lambda t: t.reshape(b, n, HEADS, DIM_HEAD).transpose(0, 2, 1, 3)
            q, k, v = (to_heads(q), to_heads(k), to_heads(v))
            q = l2norm(q) * qs
            k = l2norm(k) * ksc
            q, k = rotary_xpos(q, k)
            o = local_attention(q, k, v)
            o = o.transpose(0, 2, 1, 3).reshape(b, n, INNER)
            x = x + o @ wo
            h = shift_token(x)
            mu = h.mean(-1, keepdims=True)
            var = h.var(-1, keepdims=True)
            h = (h - mu) / jnp.sqrt(var + 1e-05) * lg + lb
            h = h @ w1 + b1
            a, g = jnp.split(h, 2, axis=-1)
            h = a * jax.nn.gelu(g, approximate=False)
            x = x + h @ w2 + b2
            return x
        key = jax.random.key(seed)
        ks = jax.random.split(key, 6)
        return {'x': jax.random.normal(ks[0], (B, N, DIM), jnp.float32), 'wqkv': jax.random.normal(ks[1], (DEPTH, DIM, 3 * INNER), jnp.float32) * 0.02, 'q_scale': jnp.ones((DEPTH, DIM_HEAD), jnp.float32), 'k_scale': jnp.ones((DEPTH, DIM_HEAD), jnp.float32), 'wo': jax.random.normal(ks[2], (DEPTH, INNER, DIM), jnp.float32) * 0.02, 'ln_g': jnp.ones((DEPTH, DIM), jnp.float32), 'ln_b': jnp.zeros((DEPTH, DIM), jnp.float32), 'w1': jax.random.normal(ks[3], (DEPTH, DIM, 2 * HID), jnp.float32) * 0.02, 'b1': jnp.zeros((DEPTH, 2 * HID), jnp.float32), 'w2': jax.random.normal(ks[4], (DEPTH, HID, DIM), jnp.float32) * 0.02, 'b2': jnp.zeros((DEPTH, DIM), jnp.float32)}
    _L0_ffn_in = _L0_ffn_setup()
    _L0_c = _w((lambda *s: np.random.randn(*s).astype(np.float32) * 0.05)(4, 128))
    _L0_wmod = _w((lambda *s: np.random.randn(*s).astype(np.float32) * 0.05)(128, 6 * 128) * 128 ** (-0.5))
    _d = {'L0_attn_hidden': _L0_attn_in['hidden'], 'L0_attn_norm1_w': _L0_attn_in['norm1_w'], 'L0_attn_norm2_w': _L0_attn_in['norm2_w'], 'L0_attn_g_wq': _L0_attn_in['g_wq'], 'L0_attn_g_kv_down': _L0_attn_in['g_kv_down'], 'L0_attn_g_k_up': _L0_attn_in['g_k_up'], 'L0_attn_g_v_up': _L0_attn_in['g_v_up'], 'L0_attn_g_wo': _L0_attn_in['g_wo'], 'L0_attn_l_wq': _L0_attn_in['l_wq'], 'L0_attn_l_wk': _L0_attn_in['l_wk'], 'L0_attn_l_wv': _L0_attn_in['l_wv'], 'L0_attn_l_wo': _L0_attn_in['l_wo'], 'L0_ffn_wqkv': _L0_ffn_in['wqkv'], 'L0_ffn_q_scale': _L0_ffn_in['q_scale'], 'L0_ffn_k_scale': _L0_ffn_in['k_scale'], 'L0_ffn_wo': _L0_ffn_in['wo'], 'L0_ffn_ln_g': _L0_ffn_in['ln_g'], 'L0_ffn_ln_b': _L0_ffn_in['ln_b'], 'L0_ffn_w1': _L0_ffn_in['w1'], 'L0_ffn_b1': _L0_ffn_in['b1'], 'L0_ffn_w2': _L0_ffn_in['w2'], 'L0_ffn_b2': _L0_ffn_in['b2'], 'L0_c': _L0_c, 'L0_wmod': _L0_wmod}
    _x0 = _d['L0_attn_hidden']
    _d['L0_attn_hidden'] = jax.random.normal(jax.random.fold_in(jax.random.key(seed), 1), (4, 1024, 128), dtype=_x0.dtype)
    del _x0
    return _d

def reference(L0_attn_hidden, L0_attn_norm1_w, L0_attn_norm2_w, L0_attn_g_wq, L0_attn_g_kv_down, L0_attn_g_k_up, L0_attn_g_v_up, L0_attn_g_wo, L0_attn_l_wq, L0_attn_l_wk, L0_attn_l_wv, L0_attn_l_wo, L0_ffn_wqkv, L0_ffn_q_scale, L0_ffn_k_scale, L0_ffn_wo, L0_ffn_ln_g, L0_ffn_ln_b, L0_ffn_w1, L0_ffn_b1, L0_ffn_w2, L0_ffn_b2, L0_c, L0_wmod):

    def _L0_attn_ref(hidden, norm1_w, norm2_w, g_wq, g_kv_down, g_k_up, g_v_up, g_wo, l_wq, l_wk, l_wv, l_wo):
        import jax, jax.numpy as jnp
        import numpy as np
        D = 128
        H = 16
        KVH = 4
        HD = D // H
        LAT = 32
        WIN = 32
        B, S = (1, 256)
        BASE_G, BASE_L = (1000000.0, 10000.0)
        EPS = 1e-06

        def rmsnorm(x, w):
            return x * jax.lax.rsqrt(jnp.mean(x * x, axis=-1, keepdims=True) + EPS) * w

        def qk_norm(x):
            return x * jax.lax.rsqrt(jnp.mean(x * x, axis=-1, keepdims=True) + EPS)

        def rope(x, base):
            s, hd = (x.shape[-2], x.shape[-1])
            inv_freq = 1.0 / base ** (jnp.arange(0, hd, 2, dtype=jnp.float32) / hd)
            freqs = jnp.arange(s, dtype=jnp.float32)[:, None] * inv_freq[None, :]
            cos, sin = (jnp.cos(freqs), jnp.sin(freqs))
            xe, xo = (x[..., ::2], x[..., 1::2])
            out = jnp.stack([xe * cos - xo * sin, xe * sin + xo * cos], axis=-1)
            return out.reshape(x.shape)

        def split_heads(x, n_heads):
            b, s, _ = x.shape
            return x.reshape(b, s, n_heads, HD).transpose(0, 2, 1, 3)

        def repeat_kv(x):
            return jnp.repeat(x, H // KVH, axis=1)

        def sdpa(q, k, v, mask):
            scores = jnp.einsum('bhqd,bhkd->bhqk', q, k) / np.sqrt(HD).astype(np.float32)
            scores = jnp.where(mask, scores, jnp.float32(-1e+30))
            probs = jax.nn.softmax(scores, axis=-1)
            return jnp.einsum('bhqk,bhkd->bhqd', probs, v)

        def merge_heads(x):
            b, h, s, hd = x.shape
            return x.transpose(0, 2, 1, 3).reshape(b, s, h * hd)

        def global_latent_attn(x, wq, w_kv_down, w_k_up, w_v_up, wo):
            q = split_heads(x @ wq, H)
            latent = x @ w_kv_down
            k = split_heads(latent @ w_k_up, KVH)
            v = split_heads(latent @ w_v_up, KVH)
            q, k = (rope(q, BASE_G), rope(k, BASE_G))
            q, k = (qk_norm(q), qk_norm(k))
            k, v = (repeat_kv(k), repeat_kv(v))
            i = jnp.arange(x.shape[1])
            causal = i[:, None] >= i[None, :]
            return merge_heads(sdpa(q, k, v, causal)) @ wo

        def local_gqa_attn(x, wq, wk, wv, wo):
            q = split_heads(x @ wq, H)
            k = split_heads(x @ wk, KVH)
            v = split_heads(x @ wv, KVH)
            q, k = (rope(q, BASE_L), rope(k, BASE_L))
            q, k = (qk_norm(q), qk_norm(k))
            k, v = (repeat_kv(k), repeat_kv(v))
            i = jnp.arange(x.shape[1])
            diff = i[:, None] - i[None, :]
            mask = (diff >= 0) & (diff < WIN)
            return merge_heads(sdpa(q, k, v, mask)) @ wo
        x = hidden
        x = x + global_latent_attn(rmsnorm(x, norm1_w), g_wq, g_kv_down, g_k_up, g_v_up, g_wo)
        x = x + local_gqa_attn(rmsnorm(x, norm2_w), l_wq, l_wk, l_wv, l_wo)
        return x

    def _L0_ffn_ref(x, wqkv, q_scale, k_scale, wo, ln_g, ln_b, w1, b1, w2, b2):
        import jax, jax.numpy as jnp
        import numpy as np
        DIM = 128
        DEPTH = 2
        HEADS = 8
        DIM_HEAD = 64
        WINDOW = 64
        INNER = HEADS * DIM_HEAD
        HID = int(DIM * 4 * 2 / 3)
        B, N = (2, 1024)
        QK_SCALE = 8.0

        def shift_token(t):
            t1, t2 = jnp.split(t, 2, axis=-1)
            t2 = jnp.pad(t2, ((0, 0), (1, 0), (0, 0)))[:, :-1]
            return jnp.concatenate([t1, t2], axis=-1)

        def l2norm(t):
            return t / jnp.clip(jnp.linalg.norm(t, axis=-1, keepdims=True), 1e-12)

        def rotate_half(x):
            x1, x2 = jnp.split(x, 2, axis=-1)
            return jnp.concatenate([-x2, x1], axis=-1)

        def rotary_xpos(q, k):
            n = q.shape[-2]
            half_idx = jnp.arange(0, DIM_HEAD, 2, dtype=jnp.float32)
            inv_freq = 1.0 / 10000.0 ** (half_idx / DIM_HEAD)
            t = jnp.arange(n, dtype=jnp.float32)
            freqs = t[:, None] * inv_freq[None, :]
            freqs = jnp.concatenate([freqs, freqs], axis=-1)
            base = (half_idx + 0.4 * DIM_HEAD) / (1.4 * DIM_HEAD)
            power = (t - n // 2) / float(WINDOW // 2)
            scale = base[None, :] ** power[:, None]
            scale = jnp.concatenate([scale, scale], axis=-1)
            cos, sin = (jnp.cos(freqs), jnp.sin(freqs))
            q = q * cos * scale + rotate_half(q) * sin * scale
            k = k * cos / scale + rotate_half(k) * sin / scale
            return (q, k)

        def local_attention(q, k, v):
            b, h, n, d = q.shape
            w = n // WINDOW
            bq = q.reshape(b, h, w, WINDOW, d) * QK_SCALE
            bk = k.reshape(b, h, w, WINDOW, d)
            bv = v.reshape(b, h, w, WINDOW, d)

            def look_around(t):
                p = jnp.pad(t, ((0, 0), (0, 0), (1, 0), (0, 0), (0, 0)))
                return jnp.concatenate([p[:, :, :w], p[:, :, 1:]], axis=3)
            bk, bv = (look_around(bk), look_around(bv))
            bt = jnp.arange(n).reshape(w, WINDOW)
            btp = jnp.pad(bt, ((1, 0), (0, 0)), constant_values=-1)
            btk = jnp.concatenate([btp[:w], btp[1:]], axis=1)
            sim = jnp.einsum('bhwid,bhwjd->bhwij', bq, bk)
            i = bt[:, :, None]
            j = btk[:, None, :]
            mask = (i < j) | (i > j + WINDOW) | (j == -1)
            sim = jnp.where(mask, -jnp.finfo(sim.dtype).max, sim)
            attn = jax.nn.softmax(sim, axis=-1)
            out = jnp.einsum('bhwij,bhwjd->bhwid', attn, bv)
            return out.reshape(b, h, n, d)

        def _layer(x, wqkv, qs, ksc, wo, lg, lb, w1, b1, w2, b2):
            b, n, _ = x.shape
            h = shift_token(x)
            qkv = h @ wqkv
            q, k, v = jnp.split(qkv, 3, axis=-1)
            to_heads = lambda t: t.reshape(b, n, HEADS, DIM_HEAD).transpose(0, 2, 1, 3)
            q, k, v = (to_heads(q), to_heads(k), to_heads(v))
            q = l2norm(q) * qs
            k = l2norm(k) * ksc
            q, k = rotary_xpos(q, k)
            o = local_attention(q, k, v)
            o = o.transpose(0, 2, 1, 3).reshape(b, n, INNER)
            x = x + o @ wo
            h = shift_token(x)
            mu = h.mean(-1, keepdims=True)
            var = h.var(-1, keepdims=True)
            h = (h - mu) / jnp.sqrt(var + 1e-05) * lg + lb
            h = h @ w1 + b1
            a, g = jnp.split(h, 2, axis=-1)
            h = a * jax.nn.gelu(g, approximate=False)
            x = x + h @ w2 + b2
            return x
        for l in range(DEPTH):
            x = _layer(x, wqkv[l], q_scale[l], k_scale[l], wo[l], ln_g[l], ln_b[l], w1[l], b1[l], w2[l], b2[l])
        return x
    x = L0_attn_hidden
    mod = (_silu(L0_c) @ L0_wmod).reshape(L0_c.shape[0], 6, 1, -1)
    sa, ca, ga, sb, cb, gb = (mod[:, 0], mod[:, 1], mod[:, 2], mod[:, 3], mod[:, 4], mod[:, 5])
    ga = (2 * (ga >= 0) - 1) * jnp.maximum(jnp.abs(ga), 0.25)
    gb = (2 * (gb >= 0) - 1) * jnp.maximum(jnp.abs(gb), 0.25)
    h = _layernorm(x, axis=-1) * (1 + ca) + sa
    x = x + ga * _L0_attn_ref(h, L0_attn_norm1_w, L0_attn_norm2_w, L0_attn_g_wq, L0_attn_g_kv_down, L0_attn_g_k_up, L0_attn_g_v_up, L0_attn_g_wo, L0_attn_l_wq, L0_attn_l_wk, L0_attn_l_wv, L0_attn_l_wo)
    h = _layernorm(x, axis=-1) * (1 + cb) + sb
    x = x + gb * _L0_ffn_ref(h, L0_ffn_wqkv, L0_ffn_q_scale, L0_ffn_k_scale, L0_ffn_wo, L0_ffn_ln_g, L0_ffn_ln_b, L0_ffn_w1, L0_ffn_b1, L0_ffn_w2, L0_ffn_b2)
    return x

_drawn_inputs = setup_inputs


def setup_inputs(seed=0):
    import zlib

    import numpy as np

    out = dict(_drawn_inputs(seed))
    spreads = {'L0_attn_norm1_w': (1.0, 0.6),
     'L0_attn_norm2_w': (1.0, 0.6),
     'L0_ffn_q_scale': (1.0, 0.6),
     'L0_ffn_k_scale': (1.0, 0.6),
     'L0_ffn_ln_g': (1.0, 0.6),
     'L0_ffn_ln_b': (0.0, 0.8),
     'L0_ffn_b1': (0.0, 0.8),
     'L0_ffn_b2': (0.0, 0.8)}
    factors = {'L0_attn_g_wq': 8.0,
     'L0_attn_g_kv_down': 8.0,
     'L0_attn_g_k_up': 8.0,
     'L0_attn_g_v_up': 8.0,
     'L0_attn_g_wo': 8.0,
     'L0_attn_l_wq': 8.0,
     'L0_attn_l_wk': 8.0,
     'L0_attn_l_wv': 8.0,
     'L0_attn_l_wo': 8.0,
     'L0_ffn_wqkv': 8.0,
     'L0_ffn_wo': 8.0,
     'L0_ffn_w1': 8.0,
     'L0_ffn_w2': 8.0}
    for name, (base, spread) in spreads.items():
        noise = np.random.default_rng([zlib.crc32(name.encode()), seed]).standard_normal(out[name].shape)
        drawn = base * np.exp(spread * noise) if base else spread * noise
        out[name] = jnp.asarray(drawn.astype(out[name].dtype))
    for name, factor in factors.items():
        out[name] = (out[name] * factor).astype(out[name].dtype)
    return out
```

```python
from contextlib import ExitStack

import numpy as np

import concourse.bass as bass
from concourse import mybir

F32 = mybir.dt.float32
F32R = mybir.dt.float32r
BF16 = mybir.dt.bfloat16
ALU = mybir.AluOpType
ACT = mybir.ActivationFunctionType
AX = mybir.AxisListType.X

P = 128
B, S, D = 4, 1024, 128
TILES = S // P
BANK = 512

HEADS, KV_HEADS, HEAD_DIM = 16, 4, 8
GROUP = HEADS // KV_HEADS
PAIRS = HEAD_DIM // 2
QK_HEADS = HEADS + KV_HEADS
QK_COLS = HEAD_DIM * QK_HEADS
V_COLS = KV_HEADS * HEAD_DIM
QKV_COLS = QK_COLS + V_COLS
LATENT = 32
WINDOW_A = 32
SPAN_A = P + WINDOW_A
V_PAD = 32
ROPE_BASES = (1e6, 1e4)
ATT_EPS = 1e-6
LN_EPS = 1e-5

DEPTH, FH, FD = 2, 8, 64
INNER = FH * FD
WIN = 64
SPAN_F = P + WIN
HID = 341
HID_BLOCKS = [(0, 128), (128, 128), (256, 85)]
QK_SCALE = 8.0
F_EPS = 1e-5
VF_STRIDE = FD + 1
VF_MOVE = 96
VF_COLS = (FH - 1) * VF_STRIDE + VF_MOVE


class Chain:

    def __init__(self, engine, steps):
        self.engine, self.steps, self.counts = engine, steps, {}
        self.last = steps

    def did(self, instruction, signal=None):
        self.last = self.steps if signal is None else signal
        self.counts[self.last] = self.counts.get(self.last, 0) + 1
        instruction.then_inc(self.last, 1)

    def settle(self):
        self.engine.wait_ge(self.last, self.counts[self.last])


class Scope:

    def __init__(self, nc, prefix):
        self.nc, self.prefix, self.stack, self.sems = nc, prefix, ExitStack(), []

    def __enter__(self):
        self.stack.__enter__()
        return self

    def __exit__(self, *exc):
        return self.stack.__exit__(*exc)

    def sb(self, name, shape, dtype=F32):
        return self.stack.enter_context(self.nc.sbuf_tensor(f"{self.prefix}_{name}", shape, dtype))

    def sem(self, name):
        s = self.stack.enter_context(self.nc.semaphore(f"{self.prefix}_{name}"))
        self.sems.append(s)
        return s

    def clear_semaphores(self):
        with self.nc.Block() as block:
            @block.sync
            def _(sp):
                for s in self.sems:
                    sp.sem_clear(s)


def flat(t):
    return t.rearrange("p a b -> p (a b)")


def widen(ap, shape):
    return ap.to_broadcast(shape)


def prepare(nc, psum, dram, keep):
    with Scope(nc, "prep") as k:
        loaded, dve_steps, act_steps = k.sem("loaded"), k.sem("dve_steps"), k.sem("act_steps")
        folded_in_psum, sig_ready, table_ready = k.sem("folded"), k.sem("sig"), k.sem("table")
        kv_up = k.sb("kv_up", [LATENT, 2 * V_COLS])
        kv_down_t = k.sb("kv_down_t", [LATENT, D])
        cond = k.sb("cond", [D, B])
        sig = k.sb("sig", [D, B])
        loads = [
            (keep.ident[:], dram["identity"]), (keep.eps[:], dram["eps"]),
            (keep.wmod[:], dram["wmod"]),
            (keep.w_qkv[0][:, 0:QK_COLS].rearrange("p (d h) -> p d h", h=QK_HEADS)[:, :, 0:HEADS],
             dram["g_wq"]),
            (keep.w_qkv[1][:], dram["l_wqkv"]),
            (keep.w_o[0][:], dram["g_wo"]), (keep.w_o[1][:], dram["l_wo"]),
            (keep.norm_w[:], dram["norm_w"]),
            (keep.rope_a[:], dram["rope_a"]), (keep.local_mask[:], dram["local_mask"]),
            (keep.causal_mask[:], dram["causal_mask"]),
            (kv_up[:], dram["kv_up"]), (kv_down_t[:], dram["kv_down_t"]), (cond[:], dram["cond"]),
        ]
        with nc.Block() as block:
            @block.sync
            def _(sp):
                for dst, src in loads:
                    sp.dma_start(dst, src).then_inc(loaded, 16)

            @block.tensor
            def _(pe):
                pe.wait_ge(loaded, 16 * len(loads))
                nc.tensor.matmul(psum[:, 0:2 * V_COLS], kv_down_t[:], kv_up[:],
                                 start=True, stop=True).then_inc(folded_in_psum, 1)

            @block.scalar
            def _(act):
                act.wait_ge(loaded, 16 * len(loads))
                act.activation(sig[:], cond[:], ACT.Exp, scale=-1.0).then_inc(sig_ready, 1)

            @block.vector
            def _(dve):
                c = Chain(dve, dve_steps)
                dve.wait_ge(loaded, 16 * len(loads))
                c.did(nc.vector.tensor_copy(keep.ident_bf[:], keep.ident[:]))
                dve.wait_ge(sig_ready, 1)
                c.did(nc.vector.tensor_scalar_add(sig[:], sig[:], 1.0))
                c.settle()
                c.did(nc.vector.reciprocal(sig[:], sig[:]))
                c.settle()
                c.did(nc.vector.tensor_tensor(keep.silu[:], cond[:], sig[:], ALU.mult))
                dve.wait_ge(folded_in_psum, 1)
                k_cols = keep.w_qkv[0][:, 0:QK_COLS].rearrange("p (d h) -> p d h", h=QK_HEADS)
                c.did(nc.vector.tensor_copy(k_cols[:, :, HEADS:QK_HEADS],
                                            psum[:, 0:V_COLS].rearrange("p (d h) -> p d h", h=KV_HEADS)))
                c.did(nc.vector.tensor_copy(keep.w_qkv[0][:, QK_COLS:QKV_COLS], psum[:, V_COLS:2 * V_COLS]))

            @block.gpsimd
            def _(pool):
                pool.memset(keep.xs[:], 0.0)
        k.clear_semaphores()


def attention_batch(nc, psum, dram, keep, k, b):
    sb, sem = k.sb, k.sem
    x, h, nrm, tmp = (sb(n, [P, TILES, D]) for n in ("x", "h", "nrm", "tmp"))
    ht = sb("ht", [P, S])
    qk = sb("qk", [P, TILES, QK_COLS])
    rot, rot2 = sb("rot", [P, TILES, QK_COLS]), sb("rot2", [P, TILES, QK_COLS])
    ssq, rnorm = sb("ssq", [P, TILES, QK_HEADS]), sb("rnorm", [P, TILES, QK_HEADS])
    stats, mv, rstd = sb("stats", [P, TILES, 6]), sb("mv", [P, TILES, 2]), sb("rstd", [P, TILES, 1])
    cond_rep, mod, gate_tmp = sb("cond_rep", [P, P]), sb("mod", [P, 6 * D]), sb("gate", [P, 2, D])
    q_hi, q_lo = sb("q_hi", [P, S], F32R), sb("q_lo", [P, S], F32R)
    k_hi, k_lo = sb("k_hi", [V_COLS, S], F32R), sb("k_lo", [V_COLS, S], F32R)
    q_stack = sb("q_stack", [P, 2, S], F32R)
    k_stack, v = k.k_stack, k.v
    E_BUFS = 4
    probs = sb("probs", [P, E_BUFS, GROUP, BANK])
    o_t = sb("o_t", [P, S])
    o_rec = sb("o_rec", [P, TILES // 2, GROUP])
    o = sb("o", [P, TILES, D])

    x_loaded = sem("x_loaded")
    cond_rep_ready, mod_in_psum, mod_copied = sem("cond_rep"), sem("mod_in_psum"), sem("mod_copied")
    mv_ready, rstd_ready = sem("mv_ready"), sem("rstd_ready")
    h_ready, sq_ready, ssum_ready, rms_ready = sem("h_ready"), sem("sq_ready"), sem("ssum"), sem("rms")
    xr_ready, xrt_in_psum, ht_ready = sem("xr_ready"), sem("xrt_in_psum"), sem("ht_ready")
    qkv_in_psum, qk_sq_ready, qk_ssq_ready, rnorm_ready = (
        sem("qkv_in_psum"), sem("qk_sq"), sem("qk_ssq"), sem("rnorm"))
    qk_copied, v_ready, rot_ready, qkt_in_psum = sem("qk_copied"), sem("v_ready"), sem("rot_ready"), sem("qkt_in_psum")
    hi_ready, lo_ready = sem("hi_ready"), sem("lo_ready")
    gathered = [sem("gathered0"), sem("gathered1")]
    scores_done, exp_done, masked, pv_done = sem("scores"), sem("exp"), sem("masked"), sem("pv")
    ot_in_psum, ot_copied, o_in_psum, o_ready = sem("ot"), sem("ot_copied"), sem("o"), sem("o_ready")
    onT_in_psum, onT_copied, wo_in_psum = sem("onT"), sem("onT_copied"), sem("wo")
    n_ready, nt_in_psum = sem("n_ready"), sem("nt")
    act_steps, dve_steps = sem("act_steps"), sem("dve_steps")

    v4 = v[:].rearrange("p t (g c) -> p t g c", g=KV_HEADS)
    ps2 = lambda bank: psum[:, bank * BANK:(bank + 2) * BANK]
    qkv_tiles = psum[:, 2 * BANK:6 * BANK].rearrange("p (t c) -> p t c", t=TILES)
    qk_ps = qkv_tiles[:, :, 0:QK_COLS]

    CHUNK = BANK
    def units(a):
        out = []
        for g in range(KV_HEADS):
            if a == 0:
                for c in range(S // CHUNK):
                    for kt in range((c + 1) * CHUNK // P):
                        q0 = max(kt * P, c * CHUNK)
                        out.append((g, kt, q0, (c + 1) * CHUNK - q0, c))
            else:
                for kt in range(TILES):
                    out.append((g, kt, kt * P, min(SPAN_A, S - kt * P), kt // 4))
        return out
    UNITS = [units(0), units(1)]
    STEPS = [2, 1]
    unit0 = [0, len(UNITS[0])]
    step0 = [0, STEPS[0] * len(UNITS[0])]
    n_chunks = KV_HEADS * 2

    def is_masked(a, unit):
        return a == 1 or unit[2] == unit[1] * P

    masked_before = [[sum(is_masked(i, u) for i in range(a) for u in UNITS[i]) +
                      sum(is_masked(a, u) for u in UNITS[a][:n]) for n in range(len(UNITS[a]))]
                     for a in range(2)]

    def opens_bank(a, kt, ch, cc):
        return (kt == 0 and ch == cc) if a == 0 or cc == 0 else kt == 3

    block = nc.Block()
    block.__enter__()

    @block.sync
    def _(sp):
        sp.dma_start(x[:], dram["hidden"][b]).then_inc(x_loaded, 16)
        for a in range(2):
            for g in range(KV_HEADS):
                slot = g % 2
                n = a * KV_HEADS + g
                if g == 0:
                    sp.wait_ge(hi_ready, 2 * (a + 1))
                    sp.wait_ge(lo_ready, 2 * (a + 1))
                if n >= 2:
                    per = [len([u for u in UNITS[i] if u[0] == 0]) * STEPS[i] for i in range(2)]
                    m = n - 2
                    done = min(m + 1, KV_HEADS) * per[0] + max(m + 1 - KV_HEADS, 0) * per[1]
                    sp.wait_ge(scores_done, done)
                rows = slice(g * P // KV_HEADS, (g + 1) * P // KV_HEADS)
                for blk, src in enumerate((q_hi, q_hi, q_lo, q_lo)):
                    sp.dma_start(q_stack[32 * blk:32 * blk + 32, slot, :].bitcast(F32),
                                 src[rows, :].bitcast(F32)).then_inc(gathered[slot], 16)
                krows = slice(g * HEAD_DIM, (g + 1) * HEAD_DIM)
                for head in range(GROUP):
                    for blk, src in enumerate((k_hi, k_lo, k_hi, k_lo)):
                        r = 32 * blk + HEAD_DIM * head
                        sp.dma_start(k_stack[r:r + HEAD_DIM, slot, head, :].bitcast(F32),
                                     src[krows, :].bitcast(F32)).then_inc(gathered[slot], 16)

    PER_GATHER = 16 * (4 + 4 * GROUP)

    @block.tensor
    def _(pe):
        pe.wait_ge(cond_rep_ready, 1)
        for i in range(2):
            ins = nc.tensor.matmul(psum[:, i * BANK:i * BANK + 3 * D], cond_rep[:],
                                   keep.wmod[:, i * 3 * D:(i + 1) * 3 * D], start=True, stop=True)
        ins.then_inc(mod_in_psum, 1)
        pe.wait_ge(mod_copied, 1)
        for a in range(2):
            pe.wait_ge(xr_ready, a + 1)
            for t in range(TILES):
                ins = nc.tensor.transpose(psum[:, t * P:(t + 1) * P], nrm[:, t, :], keep.ident[:])
                if t % 4 == 3:
                    ins.then_inc(xrt_in_psum, 1)
            for t in range(TILES):
                if t % 4 == 0:
                    pe.wait_ge(ht_ready, 2 * a + t // 4 + 1)
                ins = nc.tensor.matmul(qkv_tiles[:, t, 0:QKV_COLS], ht[:, t * P:(t + 1) * P],
                                       keep.w_qkv[a][:], start=True, stop=True)
            ins.then_inc(qkv_in_psum, 1)
            pe.wait_ge(rot_ready, a + 1)
            for t in range(TILES):
                nc.tensor.transpose(psum[:, t * P:(t + 1) * P], rot2[:, t, 0:P], keep.ident[:])
            for t in range(TILES):
                ins = nc.tensor.transpose(psum[0:V_COLS, 6 * BANK + t * P:6 * BANK + (t + 1) * P],
                                          rot2[:, t, P:QK_COLS], keep.ident[:])
            ins.then_inc(qkt_in_psum, 1)
            pe.wait_ge(v_ready, a + 1)

            def back_transpose(i):
                pe.wait_ge(ot_copied, a * n_chunks + i + 1)
                if i >= 2:
                    pe.wait_ge(o_ready, a * n_chunks + i - 1)
                cc = i % 2
                for t in range(4):
                    ins = nc.tensor.transpose(psum[:, (6 + cc) * BANK + t * P:(6 + cc) * BANK + (t + 1) * P],
                                              o_t[:, cc * BANK + t * P:cc * BANK + (t + 1) * P], keep.ident[:])
                ins.then_inc(o_in_psum, 1)

            def values(n):
                g, kt, q0, width, ch = UNITS[a][n]
                pe.wait_ge(exp_done, step0[a] + (n + 1) * STEPS[a])
                if is_masked(a, UNITS[a][n]):
                    pe.wait_ge(masked, masked_before[a][n] + 1)
                if opens_bank(a, kt, ch, 0) and g >= 1:
                    pe.wait_ge(ot_copied, a * n_chunks + 2 * g - 1)
                if opens_bank(a, kt, ch, 1) and g >= 1:
                    pe.wait_ge(ot_copied, a * n_chunks + 2 * g)
                parts = []
                for cc in range(2):
                    lo, hi = max(q0, cc * BANK), min(q0 + width, (cc + 1) * BANK)
                    if lo < hi:
                        parts.append((cc, lo, hi))
                for cc, lo, hi in parts:
                    opens = opens_bank(a, kt, ch, cc)
                    closes = kt == (4 * cc + 3)
                    for head in range(GROUP):
                        ins = nc.tensor.matmul(
                            psum[32 * head:32 * head + V_PAD, (4 + cc) * BANK + lo - cc * BANK:
                                 (4 + cc) * BANK + hi - cc * BANK],
                            v[:, kt, g * V_PAD:(g + 1) * V_PAD],
                            probs[:, (unit0[a] + n) % E_BUFS, head, lo - q0:hi - q0],
                            start=opens, stop=closes, skip_group_check=True)
                ins.then_inc(pv_done, 1)

            n_units = len(UNITS[a])
            pending = []
            done_chunks = 0
            LAG = 2
            for n in range(n_units + LAG):
                if n < n_units:
                    g, kt, q0, width, ch = UNITS[a][n]
                    if kt == 0 and (a == 1 or ch == 0):
                        pe.wait_ge(gathered[g % 2], PER_GATHER * (2 * a + g // 2 + 1))
                    for j in range(STEPS[a]):
                        step = step0[a] + n * STEPS[a] + j
                        if step >= 2:
                            pe.wait_ge(exp_done, step - 1)
                        heads = range(2 * j, 2 * j + 2) if a == 0 else range(GROUP)
                        for i, head in enumerate(heads):
                            base = (step % 2) * 2 * BANK + i * (BANK if a == 0 else BANK // 2)
                            w = width if a == 0 else min(192, S - q0)
                            ins = nc.tensor.matmul(psum[:, base:base + w],
                                                   k_stack[:, g % 2, head, kt * P:(kt + 1) * P],
                                                   q_stack[:, g % 2, q0:q0 + w], start=True, stop=True)
                        ins.then_inc(scores_done, 1)
                if n >= LAG:
                    values(n - LAG)
                    g, kt, q0, width, ch = UNITS[a][n - LAG]
                    if pending and n - pending[0][1] >= 2:
                        back_transpose(pending.pop(0)[0])
                    if kt == 4 * ch + 3:
                        pending.append((done_chunks, n))
                        done_chunks += 1
            for i, _ in pending:
                back_transpose(i)
            pe.wait_ge(o_ready, (a + 1) * n_chunks)
            for t in range(TILES):
                ins = nc.tensor.transpose(psum[:, t * P:(t + 1) * P], o[:, t, :], keep.ident[:])
                if t % 4 == 3:
                    ins.then_inc(onT_in_psum, 1)
            for t in range(TILES):
                if t % 4 == 0:
                    pe.wait_ge(onT_copied, 2 * a + t // 4 + 1)
                ins = nc.tensor.matmul(psum[:, 2 * BANK + t * P:2 * BANK + (t + 1) * P],
                                       ht[:, t * P:(t + 1) * P], keep.w_o[a][:], start=True, stop=True)
            ins.then_inc(wo_in_psum, 1)
        pe.wait_ge(n_ready, 1)
        for t in range(TILES):
            ins = nc.tensor.transpose(psum[:, t * P:(t + 1) * P], nrm[:, t, :], keep.ident[:])
        ins.then_inc(nt_in_psum, 1)

    @block.scalar
    def _(act):
        c = Chain(act, act_steps)
        act.activation(cond_rep[:], widen(keep.silu[:, bass.ds(b, 1)], [P, P]), ACT.Copy).then_inc(cond_rep_ready, 1)
        act.wait_ge(mod_in_psum, 1)
        for i in range(2):
            ins = act.activation(mod[:, i * 3 * D:(i + 1) * 3 * D], psum[:, i * BANK:i * BANK + 3 * D], ACT.Copy)
        ins.then_inc(mod_copied, 1)

        def inverse_root(out, in_, scale, eps_col, signal):
            c.did(act.activation(out, in_, ACT.Ln, scale=scale, bias=keep.eps[:, eps_col:eps_col + 1]))
            c.settle()
            c.did(act.activation(out, out, ACT.Exp, scale=-0.5), signal)

        def layernorm_rstd(n):
            act.wait_ge(mv_ready, n)
            inverse_root(rstd[:], mv[:, :, 1:2], 1.0, 0, rstd_ready)

        layernorm_rstd(1)
        for a in range(2):
            act.wait_ge(h_ready, a + 1)
            c.did(act.activation(tmp[:], h[:], ACT.Square), sq_ready)
            act.wait_ge(ssum_ready, a + 1)
            inverse_root(rstd[:], rstd[:], 1.0 / D, 1, rms_ready)
            for i in range(2):
                act.wait_ge(xrt_in_psum, 2 * a + i + 1)
                c.did(act.activation(ht[:, i * BANK:(i + 1) * BANK], psum[:, i * BANK:(i + 1) * BANK],
                                     ACT.Copy, scale=keep.norm_w[:, a:a + 1]), ht_ready)
            act.wait_ge(qkv_in_psum, a + 1)
            c.did(act.activation(qk[:], qk_ps, ACT.Copy), qk_copied)
            c.did(act.activation(v4[:, :, :, 0:HEAD_DIM],
                                 qkv_tiles[:, :, QK_COLS:QKV_COLS].rearrange("p t (g d) -> p t g d", g=KV_HEADS),
                                 ACT.Copy), v_ready)
            act.wait_ge(qk_copied, a + 1)
            c.did(act.activation(rot2[:], qk[:], ACT.Square), qk_sq_ready)
            act.wait_ge(qk_ssq_ready, a + 1)
            inverse_root(rnorm[:], ssq[:], 1.0 / HEAD_DIM, 1, rnorm_ready)
            act.wait_ge(qkt_in_psum, a + 1)
            c.did(act.activation(k_hi[:], psum[0:V_COLS, 6 * BANK:8 * BANK], ACT.Copy), hi_ready)
            c.did(act.activation(q_hi[:], ps2(0), ACT.Copy), hi_ready)
            for n, (g, kt, q0, width, ch) in enumerate(UNITS[a]):
                for j in range(STEPS[a]):
                    step = step0[a] + n * STEPS[a] + j
                    act.wait_ge(scores_done, step + 1)
                    if unit0[a] + n >= E_BUFS and j == 0:
                        act.wait_ge(pv_done, unit0[a] + n - E_BUFS + 1)
                    buf = probs[:, (unit0[a] + n) % E_BUFS, :, :]
                    src = ps2((step % 2) * 2)
                    if a == 0:
                        dst, src = buf[:, 2 * j:2 * j + 2, 0:width], src.rearrange("p (h c) -> p h c", h=2)
                    else:
                        dst, src = buf[:, :, 0:width], src.rearrange("p (h c) -> p h c", h=GROUP)
                    act.activation(dst, src[:, :, 0:width], ACT.Exp,
                                   scale=float(1.0 / np.sqrt(np.float32(HEAD_DIM)))).then_inc(exp_done, 1)
            for i in range(2):
                act.wait_ge(onT_in_psum, 2 * a + i + 1)
                c.did(act.activation(ht[:, i * BANK:(i + 1) * BANK], psum[:, i * BANK:(i + 1) * BANK],
                                     ACT.Copy), onT_copied)
        layernorm_rstd(2)
        act.wait_ge(nt_in_psum, 1)
        for half, shift in ((slice(0, 64), 0), (slice(64, P), 1)):
            c.did(act.activation(keep.xs[half, b, shift:shift + S], psum[half, 0:S], ACT.Copy))
        c.settle()

    @block.vector
    def _(dve):
        c = Chain(dve, dve_steps)
        V = nc.vector
        dve.wait_ge(mod_copied, 1)
        m6 = mod[:].rearrange("p (i j d) -> p i j d", i=2, j=3)
        c.did(V.tensor_scalar(m6[:, :, 1, :], m6[:, :, 1, :], 1.0, None, ALU.add))
        c.did(V.tensor_scalar(gate_tmp[:], m6[:, :, 2, :], 0.0, 2.0, ALU.is_ge, ALU.mult))
        c.settle()
        for turn in range(2):
            c.did(V.scalar_tensor_tensor(m6[:, :, 2, :], gate_tmp[:], -1.0, m6[:, :, 2, :], ALU.add, ALU.mult))
            c.settle()
            if turn == 0:
                c.did(V.tensor_scalar(m6[:, :, 2, :], m6[:, :, 2, :], 0.25, None, ALU.max))
                c.settle()
        c.did(V.tensor_copy(keep.gate_b[:, b, :], mod[:, 5 * D:6 * D]))
        row = lambda i: mod[:, i * D:(i + 1) * D].rearrange("p (o d) -> p o d", o=1)

        def layernorm(src, dst, n, scale_row, shift_row):
            for t in range(TILES):
                c.did(V.bn_stats(stats[:, t, :], src[:, t, :]))
            c.settle()
            for t in range(TILES):
                ins = V.bn_aggr(mv[:, t, :], stats[:, t, :])
                c.did(ins, mv_ready if t == TILES - 1 else None)
            dve.wait_ge(rstd_ready, n)
            for t in range(TILES):
                c.did(V.tensor_scalar(dst[:, t, :], src[:, t, :], mv[:, t, 0:1], rstd[:, t, :],
                                      ALU.subtract, ALU.mult))
            c.settle()
            c.did(V.tensor_tensor(dst[:], dst[:], widen(row(scale_row), [P, TILES, D]), ALU.mult))
            c.settle()
            ins = V.tensor_tensor(dst[:], dst[:], widen(row(shift_row), [P, TILES, D]), ALU.add)
            return ins

        dve.wait_ge(x_loaded, 16)
        c.did(layernorm(x, h, 1, 1, 0), h_ready)
        for a in range(2):
            dve.wait_ge(sq_ready, a + 1)
            c.did(V.tensor_reduce(rstd[:], tmp[:], AX, ALU.add), ssum_ready)
            dve.wait_ge(rms_ready, a + 1)
            c.settle()
            c.did(V.tensor_tensor(nrm[:], h[:], widen(rstd[:], [P, TILES, D]), ALU.mult), xr_ready)
            dve.wait_ge(qk_copied, a + 1)
            by_dim = lambda ap: ap.rearrange("p t (d h) -> p t d h", h=QK_HEADS)
            cos_sin = keep.rope_a[:, a, :, :, :]
            cos = cos_sin[:, 0, :, :].rearrange("p t (d o) -> p t d o", o=1)
            sin = cos_sin[:, 1, :, :].rearrange("p t (d o) -> p t d o", o=1)
            c.did(V.tensor_tensor(by_dim(rot[:]), by_dim(qk[:]), widen(cos, [P, TILES, HEAD_DIM, QK_HEADS]),
                                  ALU.mult))
            dve.wait_ge(qk_sq_ready, a + 1)
            c.did(V.tensor_reduce(ssq[:], rot2[:].rearrange("p t (d h) -> p t h d", h=QK_HEADS), AX, ALU.add),
                  qk_ssq_ready)
            c.settle()
            for half in range(2):
                d0, d1 = half * PAIRS, (1 - half) * PAIRS
                c.did(V.tensor_tensor(by_dim(rot2[:])[:, :, d0:d0 + PAIRS, :],
                                      by_dim(qk[:])[:, :, d1:d1 + PAIRS, :],
                                      widen(sin[:, :, d0:d0 + PAIRS, :], [P, TILES, PAIRS, QK_HEADS]), ALU.mult))
            c.settle()
            c.did(V.tensor_tensor(rot[:], rot[:], rot2[:], ALU.add))
            dve.wait_ge(rnorm_ready, a + 1)
            c.settle()
            c.did(V.tensor_tensor(rot2[:].rearrange("p t (h d) -> p t d h", h=QK_HEADS), by_dim(rot[:]),
                                  widen(rnorm[:].rearrange("p t (o h) -> p t o h", o=1),
                                        [P, TILES, HEAD_DIM, QK_HEADS]), ALU.mult), rot_ready)
            dve.wait_ge(hi_ready, 2 * a + 1)
            c.did(V.tensor_tensor(k_lo[:], psum[0:V_COLS, 6 * BANK:8 * BANK], k_hi[:].bitcast(F32),
                                  ALU.subtract), lo_ready)
            dve.wait_ge(hi_ready, 2 * a + 2)
            c.did(V.tensor_tensor(q_lo[:], ps2(0), q_hi[:].bitcast(F32), ALU.subtract), lo_ready)

            pending, to_copy = [], []
            chunks = 0

            def copy_chunk(i, n):
                ch = i % 2
                dve.wait_ge(pv_done, unit0[a] + n + 1)
                if i >= 2:
                    dve.wait_ge(o_in_psum, a * n_chunks + i - 1)
                c.did(V.tensor_copy(o_t[:, ch * BANK:(ch + 1) * BANK],
                                    psum[:, (4 + ch) * BANK:(5 + ch) * BANK]), ot_copied)

            def normalise(i):
                g, cc = i // 2, i % 2
                dve.wait_ge(o_in_psum, a * n_chunks + i + 1)
                src = psum[:, (6 + cc) * BANK:(7 + cc) * BANK].rearrange("p (t h c) -> p t h c", t=4, h=GROUP)
                c.settle()
                c.did(V.reciprocal(o_rec[:], src[:, :, :, HEAD_DIM]))
                c.settle()
                dst = o[:, 4 * cc:4 * cc + 4, g * GROUP * HEAD_DIM:(g + 1) * GROUP * HEAD_DIM]
                c.did(V.tensor_tensor(dst.rearrange("p t (h d) -> p t h d", h=GROUP), src[:, :, :, 0:HEAD_DIM],
                                      widen(o_rec[:].rearrange("p t (h o) -> p t h o", o=1),
                                            [P, 4, GROUP, HEAD_DIM]), ALU.mult), o_ready)

            for n, (g, kt, q0, width, ch) in enumerate(UNITS[a]):
                if is_masked(a, UNITS[a][n]):
                    dve.wait_ge(exp_done, step0[a] + (n + 1) * STEPS[a])
                buf = probs[:, (unit0[a] + n) % E_BUFS, :, :]
                if not is_masked(a, UNITS[a][n]):
                    pass
                elif a == 1:
                    c.did(V.tensor_tensor(buf[:, :, 0:width], buf[:, :, 0:width],
                                          widen(keep.local_mask[:, 0:1, 0:width], [P, GROUP, width]),
                                          ALU.mult), masked)
                else:
                    c.did(V.tensor_tensor(buf[:, :, 0:P], buf[:, :, 0:P],
                                          widen(keep.causal_mask[:], [P, GROUP, P]), ALU.mult), masked)
                if to_copy and n - to_copy[0][1] >= 2:
                    copy_chunk(*to_copy.pop(0))
                if pending and n - pending[0][1] >= 5:
                    normalise(pending.pop(0)[0])
                if kt == 4 * ch + 3:
                    to_copy.append((chunks, n))
                    pending.append((chunks, n))
                    chunks += 1
            for i, n in to_copy:
                copy_chunk(i, n)
            for i, _ in pending:
                normalise(i)
            dve.wait_ge(wo_in_psum, a + 1)
            ps_wo = ps2(2).rearrange("p (t d) -> p t d", t=TILES)
            c.did(V.tensor_tensor(h[:], h[:], ps_wo, ALU.add), h_ready)
        c.settle()
        c.did(V.tensor_tensor(tmp[:], h[:], widen(row(2), [P, TILES, D]), ALU.mult))
        c.settle()
        c.did(V.tensor_tensor(x[:], x[:], tmp[:], ALU.add))
        c.settle()
        c.did(V.tensor_copy(keep.xres[:, b, :, :], x[:]))
        c.did(layernorm(x, nrm, 2, 4, 3), n_ready)
        c.settle()

    block.__exit__(None, None, None)
    k.clear_semaphores()


def attention_half(nc, psum, dram, keep):
    with Scope(nc, "att") as k:
        k.k_stack = k.sb("k_stack", [P, 2, GROUP, S], F32R)
        k.v = k.sb("v", [P, TILES, KV_HEADS * V_PAD])
        zeroed = k.sem("zeroed")
        with nc.Block() as block:
            @block.gpsimd
            def _(pool):
                pool.memset(k.k_stack[:].bitcast(F32), 0.0)
                pool.memset(k.v[:], 0.0).then_inc(zeroed, 1)
                pool.wait_ge(zeroed, 1)
                v4 = k.v[:].rearrange("p t (g c) -> p t g c", g=KV_HEADS)
                pool.memset(v4[:, :, :, HEAD_DIM:HEAD_DIM + 1], 1.0)
        k.clear_semaphores()
        with nc.Fori(0, B) as b:
            attention_batch(nc, psum, dram, keep, k, b)


class Kept:
    pass


def keep_tensors(nc, stack):
    keep = Kept()
    sb = lambda n, shape, dt=F32: stack.enter_context(nc.sbuf_tensor(n, shape, dt))
    keep.ident, keep.ident_bf = sb("ident", [P, P]), sb("ident_bf", [P, P], BF16)
    keep.eps = sb("epsilons", [P, 3])
    keep.wmod = sb("wmod", [P, 6 * D])
    keep.w_qkv = [sb(f"w_qkv{a}", [P, QKV_COLS]) for a in range(2)]
    keep.w_o = [sb(f"w_o{a}", [P, D]) for a in range(2)]
    keep.norm_w = sb("norm_w", [P, 2])
    keep.rope_a = sb("rope_a", [P, 2, 2, TILES, HEAD_DIM])
    keep.local_mask, keep.causal_mask = sb("local_mask", [P, 1, SPAN_A]), sb("causal_mask", [P, 1, P])
    keep.silu = sb("silu", [D, B])
    keep.gate_b = sb("gate_b", [P, B, D])
    keep.xres = sb("xres", [P, B, TILES, D])
    keep.xs = sb("xs", [P, B, S + 2])
    return keep

def load_layer(nc, dram, k, layer):
    loads = [
        (k.w_qkv[:], dram["f_wqkv"][layer]), (k.w_o[:], dram["f_wo"][layer]),
        (k.w1[:], dram["f_w1"][layer]), (k.w2[:], dram["f_w2"][layer]),
        (k.vec[:], dram["f_vec"][layer]), (k.b1[:], dram["f_b1"][layer]),
        (k.qk_scale[:], dram["f_scale"][layer]),
    ]
    loaded, tables = k.layer_loaded, k.tables_done
    with nc.Block() as block:
        @block.sync
        def _(sp):
            for dst, src in loads:
                sp.dma_start(dst, src).then_inc(loaded, 16)

        @block.vector
        def _(dve):
            dve.wait_ge(loaded, 16 * len(loads))
            h = FD // 2
            base_sin, sin = (tab[:].rearrange("p t (i d) -> p t i d", i=2) for tab in (k.base_sin, k.sin))
            scale = k.qk_scale[:].rearrange("p (o i d) -> p o i d", o=1, i=2)
            nc.vector.tensor_tensor(k.cos[:], k.base_cos[:],
                                    widen(k.qk_scale[:].rearrange("p (o d) -> p o d", o=1), [P, TILES, 2 * FD]),
                                    ALU.mult).then_inc(tables, 1)
            for lo in (0, h):
                other = h - lo
                nc.vector.tensor_tensor(sin[:, :, :, lo:lo + h], base_sin[:, :, :, lo:lo + h],
                                        widen(scale[:, :, :, other:other + h], [P, TILES, 2, h]),
                                        ALU.mult).then_inc(tables, 1)
    with nc.Block() as block:
        @block.sync
        def _(sp):
            sp.sem_clear(loaded)
            sp.sem_clear(tables)


FFN_SIGNALS = """xw_ready qk_in_psum v_in_psum sq_ready ssq_ready v_copied rn_ready roped added qk_rotated
    qkt_in_psum qkt_copied s_in_psum maxed neg_ready mt_in_psum mt_copied st_in_psum exped
    o_in_psum o_normed ot_in_psum ot_copied wo_in_psum resid_done xt_in_psum mv_ready rstd_ready
    xn_ready hn_in_psum hn_ready ag_in_psum gelu_ready u_ready y_in_psum
    act_steps dve_steps pool_steps""".split()


def ffn_batch(nc, psum, keep, k, b):
    g = k.signals
    bank = lambda i, n=1: psum[:, i * BANK:(i + n) * BANK]
    slot = BANK // 2

    def score_cols(t):
        return (WIN if t == 0 else 0), SPAN_F

    def st_width(kt):
        return min(SPAN_F, S - kt * P)

    block = nc.Block()
    block.__enter__()

    @block.tensor
    def _(pe):
        T = nc.tensor
        pe.wait_ge(g["xw_ready"], 1)
        def project(t):
            x_t = k.xw[:, t * P:(t + 1) * P]
            if t >= 2:
                pe.wait_ge(g["roped"], t - 1)
            for i in range(2):
                ins = T.matmul(bank(2 * (t % 2) + i), x_t, k.w_qkv[:, i * INNER:(i + 1) * INNER],
                               start=True, stop=True)
            ins.then_inc(g["qk_in_psum"], 1)
            if t >= 2:
                pe.wait_ge(g["v_copied"], t - 1)
            T.matmul(bank(4 + t % 2), x_t, k.w_qkv[:, 2 * INNER:3 * INNER],
                     start=True, stop=True).then_inc(g["v_in_psum"], 1)

        def qk_transposes(t):
            pe.wait_ge(g["qk_rotated"], t + 1)
            if t >= 1:
                pe.wait_ge(g["qkt_copied"], t)
            for i in range(8):
                ins = T.transpose(psum[:, 6 * BANK + i * P:6 * BANK + (i + 1) * P],
                                  k.rot[:, t % 2, i * P:(i + 1) * P], keep.ident[:])
            ins.then_inc(g["qkt_in_psum"], 1)

        LAG1 = 2
        for t in range(TILES + LAG1):
            if t >= LAG1:
                qk_transposes(t - LAG1)
            if t < TILES:
                project(t)

        pe.wait_ge(g["qkt_copied"], TILES)
        pe.wait_ge(g["v_copied"], TILES)
        for t in range(TILES + 1):
            if t < TILES:
                lo, hi = score_cols(t)
                key0 = t * P - WIN
                for hf in range(2):
                    if t >= 1:
                        pe.wait_ge(g["maxed"], 2 * t + hf - 1)
                    for i in range(4):
                        head = 4 * hf + i
                        out = psum[:, 2 * hf * BANK + i * slot + lo:2 * hf * BANK + i * slot + hi]
                        T.matmul(out, k.q_t_bf[:, head // 2, t * P:(t + 1) * P, 1],
                                 k.k_t_bf[:, head, key0 + lo:key0 + hi, 1], start=True, stop=False)
                        ins = T.matmul(out, keep.ident_bf[:], k.band_bf[:, lo:hi], start=False, stop=True)
                    ins.then_inc(g["s_in_psum"], 1)
            if t >= 1:
                pe.wait_ge(g["neg_ready"], t)
                if t >= 3:
                    pe.wait_ge(g["mt_copied"], t - 2)
                T.transpose(bank(4 + (t - 1) % 2).bitcast(BF16)[0:FH, 0:P], k.neg_max[:, t - 1, :],
                            keep.ident_bf[:]).then_inc(g["mt_in_psum"], 1)

        pe.wait_ge(g["maxed"], 2 * TILES)

        def key_scores(kt, hf):
            w = st_width(kt)
            pe.wait_ge(g["mt_copied"], min(kt + 2, TILES))
            if kt >= 1:
                pe.wait_ge(g["exped"], 2 * kt + hf - 1)
            for i in range(4):
                head = 4 * hf + i
                out = psum[:, 2 * hf * BANK + i * slot:2 * hf * BANK + i * slot + w]
                T.matmul(out, k.k_t[:, head, kt * P:(kt + 1) * P], k.q_t[:, head // 2, kt * P:kt * P + w],
                         start=True, stop=False)
                T.matmul(out, k.pick[:, head, :], k.max_t[:, kt * P:kt * P + w], start=False, stop=False)
                ins = T.matmul(out, keep.ident_bf[:], k.band_t_bf[:, 0:w], start=False, stop=True)
            ins.then_inc(g["st_in_psum"], 1)

        def value_products(t):
            for hf in range(2):
                pe.wait_ge(g["exped"], 2 * t + hf + 1)
                if t >= 1:
                    pe.wait_ge(g["o_normed"], 2 * t + hf - 1)
                for i in range(4):
                    head = 4 * hf + i
                    v0 = head * VF_STRIDE
                    c0 = (4 + hf) * BANK + i * VF_STRIDE
                    ins = T.matmul(psum[:, c0:c0 + VF_MOVE], k.probs[:, t % 3, head, 0:P],
                                   k.v[:, t, v0:v0 + VF_MOVE], start=True, stop=True)
                    if t >= 1:
                        ins = T.matmul(psum[0:WIN, c0:c0 + VF_MOVE], k.probs[:, (t - 1) % 3, head, P:SPAN_F],
                                       k.v[:, t - 1, v0:v0 + VF_MOVE], start=False, stop=True,
                                       skip_group_check=True)
                ins.then_inc(g["o_in_psum"], 1)

        def out_transposes(t):
            pe.wait_ge(g["o_normed"], 2 * t + 2)
            if t >= 1:
                pe.wait_ge(g["ot_copied"], t)
            for i in range(4):
                ins = T.transpose(psum[:, 6 * BANK + i * P:6 * BANK + (i + 1) * P],
                                  k.o[:, t % 2, i * P:(i + 1) * P], keep.ident[:])
            ins.then_inc(g["ot_in_psum"], 1)

        def project_out(c):
            pe.wait_ge(g["ot_copied"], 4 * c + 4)
            if c >= 1:
                pe.wait_ge(g["resid_done"], c)
            for i in range(4):
                ins = T.matmul(bank(7), k.w_o[:, i, :], k.o_t[:, i, :], start=i == 0, stop=i == 3)
            ins.then_inc(g["wo_in_psum"], 1)

        for kt in range(TILES + 3):
            if kt < TILES:
                key_scores(kt, 0)
                key_scores(kt, 1)
            if 1 <= kt <= TILES:
                value_products(kt - 1)
            if 2 <= kt <= TILES + 1:
                out_transposes(kt - 2)
            if kt >= 3 and (kt - 3) % 4 == 3:
                project_out((kt - 3) // 4)

        pe.wait_ge(g["exped"], 2 * TILES)
        for c in range(2):
            pe.wait_ge(g["resid_done"], c + 1)
            for i in range(4):
                t = 4 * c + i
                ins = T.transpose(psum[:, c * BANK + i * P:c * BANK + (i + 1) * P],
                                  k.xw[:, t * P:(t + 1) * P], keep.ident[:])
            ins.then_inc(g["xt_in_psum"], 1)
        for c in range(2):
            pe.wait_ge(g["xn_ready"], c + 1)
            for i in range(4):
                ins = T.transpose(psum[:, (2 + c) * BANK + i * P:(2 + c) * BANK + (i + 1) * P],
                                  k.xn[:, 4 * c + i, :], keep.ident[:])
            ins.then_inc(g["hn_in_psum"], 1)
        pe.wait_ge(g["o_normed"], 2 * TILES)

        def up(n):
            c, j = divmod(n, 3)
            pe.wait_ge(g["hn_ready"], c + 1)
            if n >= 2:
                pe.wait_ge(g["u_ready"], n - 1)
            r0, rows = HID_BLOCKS[j]
            for i in range(2):
                ins = T.matmul(psum[0:rows, (4 + 2 * (n % 2) + i) * BANK:(5 + 2 * (n % 2) + i) * BANK],
                               k.w1[:, i * HID + r0:i * HID + r0 + rows],
                               k.hn[:, c * BANK:(c + 1) * BANK], start=True, stop=True)
            ins.then_inc(g["ag_in_psum"], 1)

        def down(c):
            pe.wait_ge(g["u_ready"], 3 * c + 3)
            for j, (r0, rows) in enumerate(HID_BLOCKS):
                ins = T.matmul(bank(c), k.w2[0:rows, j, :], k.u[0:rows, c, j, :], start=j == 0, stop=j == 2)
            ins.then_inc(g["y_in_psum"], 1)

        for n in range(6):
            up(n)
            if n == 4:
                down(0)
        down(1)

    @block.scalar
    def _(act):
        c = Chain(act, g["act_steps"])

        def rotary_step(t):
            act.wait_ge(g["qk_in_psum"], t + 1)
            if t >= 1:
                act.wait_ge(g["ssq_ready"], t)
            c.did(act.activation(k.sq[:], bank(2 * (t % 2), 2), ACT.Square), g["sq_ready"])
            act.wait_ge(g["v_in_psum"], t + 1)
            v_t = k.v[:, t, 0:FH * VF_STRIDE].rearrange("p (h c) -> p h c", h=FH)
            c.did(act.activation(v_t[:, :, 0:FD], bank(4 + t % 2).rearrange("p (h d) -> p h d", h=FH),
                                 ACT.Copy), g["v_copied"])
            act.wait_ge(g["ssq_ready"], t + 1)
            if t >= 2:
                act.wait_ge(g["qk_rotated"], t - 1)
            rn = k.rnorm[:, t % 2, :]
            c.did(act.activation(rn, k.ssq[:, t % 2, :], ACT.Ln, scale=float(2 ** 20)))
            c.settle()
            c.did(act.activation(rn, rn, ACT.Exp, scale=-0.5, bias=keep.eps[:, 2:3]), g["rn_ready"])

        def copy_qkt(t):
            act.wait_ge(g["qkt_in_psum"], t + 1)
            cols = slice(t * P, (t + 1) * P)
            c.did(act.activation(k.q_t[:, :, cols], bank(6).rearrange("p (i t) -> p i t", i=4), ACT.Copy))
            for j, half in ((0, slice(0, FD)), (1, slice(FD, P))):
                dst = k.k_t[half, :, cols].rearrange("p (i j) t -> p i j t", j=2)[:, :, j, :]
                c.did(act.activation(dst, psum[half, 7 * BANK:8 * BANK].rearrange("p (i t) -> p i t", i=4),
                                     ACT.Copy), g["qkt_copied"] if j else None)

        for t in range(TILES + 2):
            if t >= 2:
                copy_qkt(t - 2)
            if t < TILES:
                rotary_step(t)
        for t in range(TILES):
            act.wait_ge(g["mt_in_psum"], t + 1)
            c.did(act.activation(k.max_t[0:FH, t * P:(t + 1) * P],
                                 bank(4 + t % 2).bitcast(BF16)[0:FH, 0:P], ACT.Copy), g["mt_copied"])
        for kt in range(TILES + 2):
            if kt < TILES:
                w = st_width(kt)
                for hf in range(2):
                    act.wait_ge(g["st_in_psum"], 2 * kt + hf + 1)
                    if kt >= 3:
                        act.wait_ge(g["o_in_psum"], 2 * (kt - 1))
                    src = bank(2 * hf, 2).rearrange("p (h c) -> p h c", h=4)
                    c.did(act.activation(k.probs[:, kt % 3, 4 * hf:4 * hf + 4, 0:w], src[:, :, 0:w], ACT.Exp,
                                         scale=QK_SCALE), g["exped"])
            if kt >= 2:
                t = kt - 2
                act.wait_ge(g["ot_in_psum"], t + 1)
                if t == 4:
                    act.wait_ge(g["wo_in_psum"], 1)
                c.did(act.activation(k.o_t[:, :, (t % 4) * P:(t % 4 + 1) * P],
                                     bank(6).rearrange("p (i t) -> p i t", i=4), ACT.Copy), g["ot_copied"])
        for i in range(2):
            act.wait_ge(g["mv_ready"], i + 1)
            r = k.rstd[:, 4 * i:4 * i + 4, :]
            c.did(act.activation(r, k.mv[:, 4 * i:4 * i + 4, 1:2], ACT.Ln, bias=keep.eps[:, 0:1]))
            c.settle()
            c.did(act.activation(r, r, ACT.Exp, scale=-0.5), g["rstd_ready"])
        for i in range(2):
            act.wait_ge(g["hn_in_psum"], i + 1)
            c.did(act.activation(k.hn[:, i * BANK:(i + 1) * BANK], bank(2 + i), ACT.Identity,
                                 scale=k.vec[:, 0:1], bias=k.vec[:, 1:2]), g["hn_ready"])
        for n in range(6):
            j = n % 3
            rows = HID_BLOCKS[j][1]
            act.wait_ge(g["ag_in_psum"], n + 1)
            if n >= 2:
                act.wait_ge(g["u_ready"], n - 1)
            c.did(act.activation(k.gelu[0:rows, n % 2, :],
                                 psum[0:rows, (5 + 2 * (n % 2)) * BANK:(6 + 2 * (n % 2)) * BANK],
                                 ACT.Gelu, bias=k.b1[0:rows, 3 + j:4 + j]), g["gelu_ready"])

    @block.gpsimd
    def _(pool):
        c = Chain(pool, g["pool_steps"])
        for t in range(TILES):
            pool.wait_ge(g["roped"], t + 1)
            c.did(pool.tensor_tensor(k.rot[:, t % 2, :], k.rot[:, t % 2, :], k.rot_sin[:, t % 2, :], ALU.add),
                  g["added"])

    @block.vector
    def _(dve):
        c = Chain(dve, g["dve_steps"])
        V = nc.vector
        c.did(V.tensor_copy(k.xw[:, 0:S + 1], keep.xs[:, b, 0:S + 1]), g["xw_ready"])

        def rope(t):
            dve.wait_ge(g["sq_ready"], t + 1)
            if t >= 2:
                dve.wait_ge(g["rn_ready"], t - 1)
            c.did(V.tensor_reduce(k.ssq[:, t % 2, :], k.sq[:].rearrange("p (h d) -> p h d", d=FD), AX, ALU.add))
            c.settle()
            c.did(V.tensor_scalar(k.ssq[:, t % 2, :], k.ssq[:, t % 2, :], 1e-24, None, ALU.max), g["ssq_ready"])
            if t >= 2:
                dve.wait_ge(g["qkt_in_psum"], t - 1)
            src = bank(2 * (t % 2), 2).rearrange("p (i h d) -> p i h d", i=2, h=FH)
            heads = lambda tab: tab.rearrange("p (i o d) -> p i o d", i=2, o=1)
            as_heads = lambda ap: ap.rearrange("p (i h d) -> p i h d", i=2, h=FH)
            c.did(V.tensor_tensor(as_heads(k.rot[:, t % 2, :]), src,
                                  widen(heads(k.cos[:, t, :]), [P, 2, FH, FD]), ALU.mult))
            for lo in (0, FD // 2):
                other = FD // 2 - lo
                c.did(V.tensor_tensor(as_heads(k.rot_sin[:, t % 2, :])[:, :, :, lo:lo + FD // 2],
                                      src[:, :, :, other:other + FD // 2],
                                      widen(heads(k.sin[:, t, :])[:, :, :, lo:lo + FD // 2],
                                            [P, 2, FH, FD // 2]), ALU.mult), g["roped"] if lo else None)

        def normalise(t):
            dve.wait_ge(g["added"], t + 1)
            dve.wait_ge(g["rn_ready"], t + 1)
            r = k.rot[:, t % 2, :].rearrange("p (h d) -> p h d", d=FD)
            c.did(V.tensor_tensor(r, r, widen(k.rnorm[:, t % 2, :].rearrange("p (h o) -> p h o", o=1),
                                              [P, 2 * FH, FD]), ALU.mult), g["qk_rotated"])

        for t in range(TILES + 1):
            if t < TILES:
                rope(t)
            if t >= 1:
                normalise(t - 1)

        for t in range(TILES):
            lo, hi = score_cols(t)
            for hf in range(2):
                dve.wait_ge(g["s_in_psum"], 2 * t + hf + 1)
                src = bank(2 * hf, 2).rearrange("p (h c) -> p h c", h=4)
                c.did(V.tensor_reduce(k.row_max[:, t, 4 * hf:4 * hf + 4], src[:, :, lo:hi], AX, ALU.max),
                      g["maxed"])
            c.settle()
            c.did(V.tensor_scalar(k.neg_max[:, t, :], k.row_max[:, t, :], -1.0, None, ALU.mult), g["neg_ready"])

        def norm_out(t):
            for hf in range(2):
                dve.wait_ge(g["o_in_psum"], 2 * t + hf + 1)
                src = psum[:, (4 + hf) * BANK:(4 + hf) * BANK + 4 * VF_STRIDE].rearrange(
                    "p (h c) -> p h c", h=4)
                rec = k.o_rec[:, 4 * hf:4 * hf + 4]
                if t >= 1:
                    c.settle()
                c.did(V.reciprocal(rec, src[:, :, FD]))
                c.settle()
                if t >= 2 and hf == 0:
                    dve.wait_ge(g["ot_in_psum"], t - 1)
                dst = k.o[:, t % 2, hf * 4 * FD:(hf + 1) * 4 * FD].rearrange("p (h d) -> p h d", h=4)
                c.did(V.tensor_tensor(dst, src[:, :, 0:FD],
                                      widen(rec.rearrange("p (h o) -> p h o", o=1), [P, 4, FD]), ALU.mult),
                      g["o_normed"])

        def add_residual(n):
            dve.wait_ge(g["wo_in_psum"], n + 1)
            for half, shift in ((slice(0, 64), 0), (slice(64, P), 1)):
                x = k.xw[half, n * BANK + shift:(n + 1) * BANK + shift]
                c.did(V.tensor_tensor(x, x, psum[half, 7 * BANK:8 * BANK], ALU.add),
                      g["resid_done"] if shift else None)

        for t in range(TILES + 3):
            if t < TILES:
                norm_out(t)
            if t >= 3 and (t - 3) % 4 == 3:
                add_residual((t - 3) // 4)

        for i in range(2):
            dve.wait_ge(g["xt_in_psum"], i + 1)
            for t in range(4):
                src = psum[:, i * BANK + t * P:i * BANK + (t + 1) * P]
                c.did(V.bn_stats(k.stats[:, 4 * i + t, :], src))
            c.settle()
            for t in range(4):
                c.did(V.bn_aggr(k.mv[:, 4 * i + t, :], k.stats[:, 4 * i + t, :]), g["mv_ready"] if t == 3 else None)
        for i in range(2):
            dve.wait_ge(g["rstd_ready"], i + 1)
            for t in range(4):
                n = 4 * i + t
                src = psum[:, i * BANK + t * P:i * BANK + (t + 1) * P]
                c.did(V.tensor_scalar(k.xn[:, n, :], src, k.mv[:, n, 0:1], k.rstd[:, n, :],
                                      ALU.subtract, ALU.mult), g["xn_ready"] if t == 3 else None)

        def gate(n):
            i, j = divmod(n, 3)
            rows = HID_BLOCKS[j][1]
            dve.wait_ge(g["gelu_ready"], n + 1)
            a = psum[0:rows, (4 + 2 * (n % 2)) * BANK:(5 + 2 * (n % 2)) * BANK]
            c.did(V.scalar_tensor_tensor(k.u[0:rows, i, j, :], a, k.b1[0:rows, j:j + 1],
                                         k.gelu[0:rows, n % 2, :], ALU.add, ALU.mult), g["u_ready"])

        def finish(n):
            dve.wait_ge(g["y_in_psum"], n + 1)
            for half, shift in ((slice(0, 64), 0), (slice(64, P), 1)):
                cols = slice(n * BANK + shift, (n + 1) * BANK + shift)
                c.did(V.scalar_tensor_tensor(keep.xs[half, b, cols], psum[half, n * BANK:(n + 1) * BANK],
                                             k.vec[half, 2:3], k.xw[half, cols], ALU.add, ALU.add))

        for n in range(6):
            gate(n)
        finish(0)
        finish(1)
        c.settle()

    block.__exit__(None, None, None)
    k.clear_semaphores()


def ffn_half(nc, psum, dram, keep):
    with Scope(nc, "ffn") as k:
        sb = k.sb
        k.w_qkv, k.w_o = sb("w_qkv", [P, 3 * INNER]), sb("w_o", [P, INNER // P, D])
        k.w1, k.w2 = sb("w1", [P, 2 * HID]), sb("w2", [P, 3, D])
        k.vec, k.b1, k.qk_scale = sb("vec", [P, 3]), sb("b1", [P, 6]), sb("qk_scale", [P, 2 * FD])
        k.base_cos, k.base_sin, k.cos, k.sin = (sb(n, [P, TILES, 2 * FD])
                                                for n in ("base_cos", "base_sin", "cos", "sin"))
        k.xw = sb("xw", [P, S + 2])
        k.rot, k.rot_sin = sb("rot", [P, 2, 2 * INNER]), sb("rot_sin", [P, 2, 2 * INNER])
        k.sq = sb("sq", [P, 2 * INNER])
        k.ssq, k.rnorm = sb("ssq", [P, 2, 2 * FH]), sb("rnorm", [P, 2, 2 * FH])
        k.q_t, k.k_t = sb("q_t", [P, FH // 2, S]), sb("k_t", [P, FH, S])
        k.q_t_bf = k.q_t[:].bitcast(BF16).rearrange("p i (t w) -> p i t w", w=2)
        k.k_t_bf = k.k_t[:].bitcast(BF16).rearrange("p i (t w) -> p i t w", w=2)
        k.v = sb("v", [P, TILES, VF_COLS])
        k.band_bf, k.band_t_bf = sb("band", [P, SPAN_F], BF16), sb("band_t", [P, SPAN_F], BF16)
        k.pick = sb("pick", [P, FH, P], BF16)
        k.row_max, k.neg_max = sb("row_max", [P, TILES, FH]), sb("neg_max", [P, TILES, FH], BF16)
        k.max_t = sb("max_t", [P, S], BF16)
        k.probs = sb("probs", [P, 3, FH, SPAN_F])
        k.o, k.o_rec, k.o_t = sb("o", [P, 2, INNER]), sb("o_rec", [P, FH]), sb("o_t", [P, INNER // P, BANK])
        k.stats, k.mv, k.rstd = sb("stats", [P, TILES, 6]), sb("mv", [P, TILES, 2]), sb("rstd", [P, TILES, 1])
        k.xn = k.sq[:].rearrange("p (t d) -> p t d", t=TILES)
        k.hn = k.rot_sin[:, 0, :]
        k.gelu = k.rot_sin[:, 1, :].rearrange("p (i c) -> p i c", i=2)
        k.u = flat(k.q_t[:])[:, 0:6 * BANK].rearrange("p (c j t) -> p c j t", c=2, j=3)
        band, band_t, pick = k.u[:, 0, 0, 0:SPAN_F], k.u[:, 0, 1, 0:SPAN_F], flat(k.u[:, 1, 0:2, :])
        loaded, zeroed = k.sem("loaded"), k.sem("zeroed")
        k.layer_loaded, k.tables_done = k.sem("layer_loaded"), k.sem("tables_done")
        k.signals = {n: k.sem(n) for n in FFN_SIGNALS}
        with nc.Block() as block:
            @block.sync
            def _(sp):
                for dst, src in ((k.base_cos[:], dram["f_cos"]), (k.base_sin[:], dram["f_sin"]),
                                 (band, dram["f_band"]),
                                 (band_t, dram["f_band_t"]), (pick, dram["f_pick"])):
                    sp.dma_start(dst, src).then_inc(loaded, 16)

            @block.gpsimd
            def _(pool):
                pool.memset(k.k_t[:], 0.0)
                pool.memset(k.max_t[:], 0.0)
                pool.memset(k.v[:], 0.0).then_inc(zeroed, 1)
                pool.wait_ge(zeroed, 1)
                ones = k.v[:, :, 0:FH * VF_STRIDE].rearrange("p t (h c) -> p t h c", h=FH)[:, :, :, FD:FD + 1]
                pool.memset(ones, 1.0)

            @block.vector
            def _(dve):
                dve.wait_ge(loaded, 80)
                nc.vector.tensor_copy(k.band_bf[:], band)
                nc.vector.tensor_copy(k.band_t_bf[:], band_t)
                nc.vector.tensor_copy(flat(k.pick[:]), pick)
        k.clear_semaphores()
        with nc.Fori(0, DEPTH) as layer:
            load_layer(nc, dram, k, layer)
            with nc.Fori(0, B) as b:
                ffn_batch(nc, psum, keep, k, b)


def write_out(nc, psum, dram, keep):
    with Scope(nc, "out") as k:
        state, y = k.sb("state", [P, S]), k.sb("y", [P, TILES, D])
        state_ready, t_in_psum, y_ready, stored = (k.sem(n) for n in ("state", "t_in_psum", "y_ready", "stored"))
        gated = k.sem("gated")
        with nc.Fori(0, B) as b:
            with nc.Block() as block:
                @block.scalar
                def _(act):
                    for half, shift in ((slice(0, 64), 0), (slice(64, P), 1)):
                        act.activation(state[half, :], keep.xs[half, b, shift:shift + S],
                                       ACT.Copy).then_inc(state_ready, 1)

                @block.tensor
                def _(pe):
                    pe.wait_ge(state_ready, 2)
                    for t in range(TILES):
                        ins = nc.tensor.transpose(psum[:, t * P:(t + 1) * P], state[:, t * P:(t + 1) * P],
                                                  keep.ident[:])
                    ins.then_inc(t_in_psum, 1)

                @block.vector
                def _(dve):
                    dve.wait_ge(t_in_psum, 1)
                    nc.vector.tensor_tensor(
                        y[:], psum[:, 0:2 * BANK].rearrange("p (t d) -> p t d", t=TILES),
                        widen(keep.gate_b[:, b, :].rearrange("p (o d) -> p o d", o=1), [P, TILES, D]),
                        ALU.mult).then_inc(gated, 1)
                    dve.wait_ge(gated, 1)
                    nc.vector.tensor_tensor(y[:], y[:], keep.xres[:, b, :, :], ALU.add).then_inc(y_ready, 1)

                @block.sync
                def _(sp):
                    sp.wait_ge(y_ready, 1)
                    sp.dma_start(dram["out"][b].rearrange("(t p) d -> p t d", p=P), y[:]).then_inc(stored, 16)
                    sp.wait_ge(stored, 16)
            k.clear_semaphores()


def build_program(nc, dram):
    with ExitStack() as stack:
        psum = stack.enter_context(nc.psum_tensor("psum", [P, 8 * BANK], F32))
        keep = keep_tensors(nc, stack)
        prepare(nc, psum, dram, keep)
        attention_half(nc, psum, dram, keep)
        ffn_half(nc, psum, dram, keep)
        write_out(nc, psum, dram, keep)



def head_columns(w, heads):
    return w.reshape(D, heads, PAIRS, 2).transpose(0, 3, 2, 1).reshape(D, HEAD_DIM, heads)


def constants():
    f = np.float32
    pos = np.arange(S, dtype=f)
    rope_a = np.zeros((2, 2, S, HEAD_DIM), f)
    for a, base in enumerate(ROPE_BASES):
        inv = f(1) / np.power(f(base), np.arange(0, HEAD_DIM, 2, dtype=f) / f(HEAD_DIM))
        ang = (pos[:, None] * inv[None, :]).astype(f)
        cos, sin = np.cos(ang), np.sin(ang)
        rope_a[a, 0] = np.concatenate([cos, cos], 1)
        rope_a[a, 1] = np.concatenate([-sin, sin], 1)
    rope_a = rope_a.reshape(2, 2, TILES, P, HEAD_DIM).transpose(3, 0, 1, 2, 4)
    key, query = np.arange(P)[:, None], np.arange(SPAN_A)[None, :]
    local = ((query >= key) & (query - key < WINDOW_A)).astype(f)
    causal = (query[:, :P] >= key).astype(f)
    half = np.arange(0, FD, 2, dtype=f)
    ang = (pos[:, None] * (f(1) / np.power(f(10000), half / f(FD)))[None, :]).astype(f)
    base = (half + f(0.4 * FD)) / f(1.4 * FD)
    xpos = np.power(base[None, :], ((pos - S // 2) / f(WIN // 2))[:, None]).astype(f)
    cos, sin = np.cos(ang), np.sin(ang)
    both = lambda q, k_: np.concatenate([q, k_], 1).reshape(TILES, P, 2 * FD).transpose(1, 0, 2)
    twice = lambda lo, hi: np.concatenate([lo, hi], 1)
    f_cos = both(twice(cos * xpos, cos * xpos), twice(cos / xpos, cos / xpos))
    f_sin = both(twice(-sin * xpos, sin * xpos), twice(-sin / xpos, sin / xpos))
    q_pos, k_pos = np.arange(P)[:, None] + WIN, np.arange(SPAN_F)[None, :]
    seen = (k_pos <= q_pos) & (k_pos >= q_pos - WIN)
    k_pos, q_pos = np.arange(P)[:, None], np.arange(SPAN_F)[None, :]
    seen_t = (k_pos <= q_pos) & (k_pos >= q_pos - WIN)
    pick = np.zeros((P, FH, P), f)
    for head in range(FH):
        pick[head, head, :] = 1
    return {
        "f_cos": f_cos, "f_sin": f_sin, "f_band": np.where(seen, f(0), f(-1e30)),
        "f_band_t": np.where(seen_t, f(0), f(-1e30)),
        "f_pick": pick.reshape(P, FH * P),
        "identity": np.eye(P, dtype=f), "rope_a": rope_a, "local_mask": local[:, None, :],
        "causal_mask": causal[:, None, :],
        "eps": np.tile(np.array([[LN_EPS, ATT_EPS, 10 * np.log(2.0)]], f), (P, 1)),
    }


def layouts(x):
    a = lambda n: np.asarray(x[f"L0_attn_{n}"])
    q_k = np.concatenate([head_columns(a("l_wq"), HEADS), head_columns(a("l_wk"), KV_HEADS)], 2)
    g_q = head_columns(a("g_wq"), HEADS)
    up = head_columns(np.pad(a("g_k_up"), ((0, D - LATENT), (0, 0))), KV_HEADS)[:LATENT]
    out = {
        "hidden": a("hidden").reshape(B, TILES, P, D).transpose(0, 2, 1, 3),
        "l_wqkv": np.concatenate([q_k.reshape(D, QK_COLS), a("l_wv")], 1),
        "g_wq": g_q, "kv_up": np.concatenate([up.reshape(LATENT, V_COLS), a("g_v_up")], 1),
        "kv_down_t": a("g_kv_down").T, "g_wo": a("g_wo"), "l_wo": a("l_wo"),
        "norm_w": np.stack([a("norm1_w"), a("norm2_w")], 1),
        "cond": np.asarray(x["L0_c"]).T, "wmod": np.asarray(x["L0_wmod"]),
    }
    w = lambda n: np.asarray(x[f"L0_ffn_{n}"])
    b1 = np.zeros((DEPTH, P, 6), np.float32)
    w2 = np.zeros((DEPTH, P, 3, D), np.float32)
    for j, (r0, rows) in enumerate(HID_BLOCKS):
        b1[:, :rows, j] = w("b1")[:, r0:r0 + rows]
        b1[:, :rows, 3 + j] = w("b1")[:, HID + r0:HID + r0 + rows]
        w2[:, :rows, j, :] = w("w2")[:, r0:r0 + rows, :]
    scale = np.concatenate([w("q_scale"), w("k_scale")], 1)
    out.update({
        "f_wqkv": w("wqkv"), "f_wo": w("wo").reshape(DEPTH, INNER // P, P, D).transpose(0, 2, 1, 3),
        "f_w1": w("w1"), "f_w2": w2, "f_b1": b1,
        "f_vec": np.stack([w("ln_g"), w("ln_b"), w("b2")], 2),
        "f_scale": np.broadcast_to(scale[:, None, :], (DEPTH, P, 2 * FD)),
    })
    return out


def kernel(**inputs):
    import concourse.bacc as bacc
    from concourse.bass_utils import run_bass_kernel_spmd

    nc = bacc.Bacc("TRN2", target_bir_lowering=False, num_devices=1)
    arrays, dram = {}, {}
    for name, value in {**layouts(inputs), **constants()}.items():
        value = np.ascontiguousarray(value)
        arrays[f"in_{name}"] = value
        dram[name] = nc.dram_tensor(f"in_{name}", value.shape, F32, kind="ExternalInput").ap()
    dram["out"] = nc.dram_tensor("out", (B, S, D), F32, kind="ExternalOutput").ap()
    build_program(nc, dram)
    result = run_bass_kernel_spmd(nc, [arrays], core_ids=[0])
    return result.results[0]["out"]
```

```python
from contextlib import ExitStack

import numpy as np

import concourse.bass as bass
from concourse import mybir

F32 = mybir.dt.float32
F32R = mybir.dt.float32r
BF16 = mybir.dt.bfloat16
ALU = mybir.AluOpType
ACT = mybir.ActivationFunctionType
AX = mybir.AxisListType.X

P = 128
B, S, D = 4, 1024, 128
TILES = S // P
BANK = 512

HEADS, KV_HEADS, HEAD_DIM = 16, 4, 8
GROUP = HEADS // KV_HEADS
PAIRS = HEAD_DIM // 2
QK_HEADS = HEADS + KV_HEADS
QK_COLS = HEAD_DIM * QK_HEADS
V_COLS = KV_HEADS * HEAD_DIM
QKV_COLS = QK_COLS + V_COLS
LATENT = 32
PAIR = 2
WINDOW_A = 32
SPAN_A = P + WINDOW_A
PARTS = 4
V_PAD = 32
ROPE_BASES = (1e6, 1e4)
ATT_EPS = 1e-6
LN_EPS = 1e-5

DEPTH, FH, FD = 2, 8, 64
INNER = FH * FD
WIN = 64
SPAN_F = P + WIN
HID = 341
HID_BLOCKS = [(0, 128), (128, 128), (256, 85)]
QK_SCALE = 8.0
F_EPS = 1e-5
VF_STRIDE = FD + 1
VF_MOVE = 96
VF_COLS = (FH - 1) * VF_STRIDE + VF_MOVE

ROOTS_AND_EXP = "natural_log_exp_and_others"


class Chain:

    def __init__(self, engine, steps):
        self.engine, self.steps, self.counts = engine, steps, {}
        self.last = steps

    def did(self, instruction, signal=None):
        self.last = self.steps if signal is None else signal
        self.counts[self.last] = self.counts.get(self.last, 0) + 1
        instruction.then_inc(self.last, 1)

    def settle(self):
        self.engine.wait_ge(self.last, self.counts[self.last])


class Scope:

    def __init__(self, nc, prefix):
        self.nc, self.prefix, self.stack, self.sems = nc, prefix, ExitStack(), []

    def __enter__(self):
        self.stack.__enter__()
        return self

    def __exit__(self, *exc):
        return self.stack.__exit__(*exc)

    def sb(self, name, shape, dtype=F32):
        return self.stack.enter_context(self.nc.sbuf_tensor(f"{self.prefix}_{name}", shape, dtype))

    def sem(self, name):
        s = self.stack.enter_context(self.nc.semaphore(f"{self.prefix}_{name}"))
        self.sems.append(s)
        return s

    def clear_semaphores(self):
        with self.nc.Block() as block:
            @block.sync
            def _(sp):
                for s in self.sems:
                    sp.sem_clear(s)


def flat(t):
    return t.rearrange("p a b -> p (a b)")


def widen(ap, shape):
    return ap.to_broadcast(shape)


def newton_step(engine, chain, out, tmp, root, x, signal):
    chain.did(engine.tensor_tensor(tmp, root, root, ALU.mult))
    chain.settle()
    chain.did(engine.tensor_tensor(tmp, tmp, x, ALU.mult))
    chain.settle()
    chain.did(engine.tensor_scalar(tmp, tmp, -0.5, 1.5, ALU.mult, ALU.add))
    chain.settle()
    chain.did(engine.tensor_tensor(out, root, tmp, ALU.mult), signal)


def prepare(nc, psum, dram, keep):
    with Scope(nc, "prep") as k:
        loaded, dve_steps, act_steps = k.sem("loaded"), k.sem("dve_steps"), k.sem("act_steps")
        folded_in_psum, sig_ready, table_ready = k.sem("folded"), k.sem("sig"), k.sem("table")
        kv_up = k.sb("kv_up", [LATENT, 2 * V_COLS])
        kv_down_t = k.sb("kv_down_t", [LATENT, D])
        cond = k.sb("cond", [D, B])
        sig = k.sb("sig", [D, B])
        loads = [
            (keep.ident[:], dram["identity"]), (keep.eps[:], dram["eps"]), (keep.part[:], dram["part"]),
            (keep.wmod[:], dram["wmod"]),
            (keep.w_qkv[0][:, 0:QK_COLS].rearrange("p (d h) -> p d h", h=QK_HEADS)[:, :, 0:HEADS],
             dram["g_wq"]),
            (keep.w_qkv[1][:], dram["l_wqkv"]),
            (keep.w_o[0][:], dram["g_wo"]), (keep.w_o[1][:], dram["l_wo"]),
            (keep.norm_w[:], dram["norm_w"]),
            (keep.rope_a[:], dram["rope_a"]), (keep.local_mask[:], dram["local_mask"]),
            (keep.causal_mask[:], dram["causal_mask"]),
            (kv_up[:], dram["kv_up"]), (kv_down_t[:], dram["kv_down_t"]), (cond[:], dram["cond"]),
        ]
        with nc.Block() as block:
            @block.sync
            def _(sp):
                for dst, src in loads:
                    sp.dma_start(dst, src).then_inc(loaded, 16)

            @block.tensor
            def _(pe):
                pe.wait_ge(loaded, 16 * len(loads))
                nc.tensor.matmul(psum[:, 0:2 * V_COLS], kv_down_t[:], kv_up[:],
                                 start=True, stop=True).then_inc(folded_in_psum, 1)

            @block.scalar
            def _(act):
                act.wait_ge(loaded, 16 * len(loads))
                act.activation(sig[:], cond[:], ACT.Exp, scale=-1.0).then_inc(sig_ready, 1)

            @block.vector
            def _(dve):
                c = Chain(dve, dve_steps)
                dve.wait_ge(loaded, 16 * len(loads))
                c.did(nc.vector.tensor_copy(keep.ident_bf[:], keep.ident[:]))
                dve.wait_ge(sig_ready, 1)
                c.did(nc.vector.tensor_scalar_add(sig[:], sig[:], 1.0))
                c.settle()
                c.did(nc.vector.reciprocal(sig[:], sig[:]))
                c.settle()
                c.did(nc.vector.tensor_tensor(keep.silu[:], cond[:], sig[:], ALU.mult))
                dve.wait_ge(folded_in_psum, 1)
                k_cols = keep.w_qkv[0][:, 0:QK_COLS].rearrange("p (d h) -> p d h", h=QK_HEADS)
                c.did(nc.vector.tensor_copy(k_cols[:, :, HEADS:QK_HEADS],
                                            psum[:, 0:V_COLS].rearrange("p (d h) -> p d h", h=KV_HEADS)))
                c.did(nc.vector.tensor_copy(keep.w_qkv[0][:, QK_COLS:QKV_COLS], psum[:, V_COLS:2 * V_COLS]))

            @block.gpsimd
            def _(pool):
                pool.memset(keep.xs[:], 0.0)
        k.clear_semaphores()


def attention_pair(nc, psum, dram, keep, k, pair):
    sb, sem = k.sb, k.sem
    h, nrm = (sb(n, [P, PAIR, TILES, D]) for n in ("h", "nrm"))
    ht = sb("ht", [P, PAIR, S])
    qk, rot2 = sb("qk", [P, PAIR, TILES, QK_COLS]), sb("rot2", [P, PAIR, TILES, QK_COLS])
    o = qk[:, :, :, 0:D]
    mean_sq, root, rnorm, refine = (sb(n, [P, PAIR, TILES, QK_HEADS]) for n in
                                    ("mean_sq", "root", "rnorm", "refine"))
    stats, mv = sb("stats", [P, PAIR, TILES, 6]), sb("mv", [P, PAIR, TILES, 2])
    row_sq, row_root, rstd, row_refine = (sb(n, [P, PAIR, TILES]) for n in
                                          ("row_sq", "row_root", "rstd", "row_refine"))
    cond_rep, mod, gate_tmp = sb("cond_rep", [P, PAIR, P]), sb("mod", [P, PAIR, 6 * D]), sb("gate", [P, PAIR, 2, D])
    q_hi, q_lo = sb("q_hi", [P, PAIR, S], F32R), sb("q_lo", [P, PAIR, S], F32R)
    k_parts = sb("k_parts", [P, PAIR, S], F32R)
    q_stack = sb("q_stack", [P, 2, S], F32R)
    k_stack, v = k.k_stack, k.v
    E_BUFS = 4
    probs = sb("probs", [P, E_BUFS, GROUP, BANK])
    scratch = flat(probs[:].rearrange("p b h c -> p b (h c)"))
    rot = scratch[:, 0:PAIR * TILES * QK_COLS].rearrange("p (e t c) -> p e t c", e=PAIR, t=TILES)
    k_rep = scratch[:, PAIR * TILES * QK_COLS:PAIR * TILES * (QK_COLS + P)].rearrange(
        "p (e t c) -> p e t c", e=PAIR, t=TILES)
    o_t = ht[:, 0]
    o_rec = sb("o_rec", [P, TILES // 2, GROUP])

    x_loaded = sem("x_loaded")
    cond_rep_ready, mod_in_psum, mod_copied = sem("cond_rep_s"), sem("mod_in_psum"), sem("mod_copied")
    x_mod_done = sem("x_mod_done")
    row_sq_ready, row_root_ready = sem("row_sq_s"), sem("row_root_s")
    h_ready, sq_ready = sem("h_ready"), sem("sq_ready")
    xr_ready, xrt_in_psum, ht_ready = sem("xr_ready"), sem("xrt_in_psum"), sem("ht_ready")
    qkv_in_psum, qk_sq_ready, mean_sq_ready = sem("qkv_in_psum"), sem("qk_sq"), sem("mean_sq_s")
    qk_root_ready, rnorm_ready = sem("qk_root"), sem("rnorm_s")
    qk_copied, v_ready, rot_ready, qkt_in_psum = sem("qk_copied"), sem("v_ready"), sem("rot_ready"), sem("qkt_in_psum")
    hi_ready, lo_ready = sem("hi_ready"), sem("lo_ready")
    gathered = [sem("gathered0"), sem("gathered1")]
    scores_done, exp_done, pv_done = sem("scores"), sem("exp"), sem("pv")
    masked, masked_rest = sem("masked"), sem("masked_rest")
    ot_copied, o_in_psum, o_ready = sem("ot_copied"), sem("o_s"), sem("o_ready")
    onT_in_psum, onT_copied, wo_in_psum = sem("onT"), sem("onT_copied"), sem("wo")
    n_ready, nt_in_psum = sem("n_ready"), sem("nt")
    act_steps, dve_steps, pool_steps = sem("act_steps"), sem("dve_steps"), sem("pool_steps")

    x = keep.xres[:].rearrange("p (q e) t d -> p q e t d", e=PAIR)[:, pair]
    state = keep.xs[:].rearrange("p (q e) s -> p q e s", e=PAIR)[:, pair]
    gate_b = keep.gate_b[:].rearrange("p (q e) d -> p q e d", e=PAIR)[:, pair]
    v4 = v[:].rearrange("p e t (g c) -> p e t g c", g=KV_HEADS)
    ps2 = lambda bank: psum[:, bank * BANK:(bank + 2) * BANK]
    qkv_tiles = psum[:, 2 * BANK:6 * BANK].rearrange("p (t c) -> p t c", t=TILES)
    qk_ps = qkv_tiles[:, :, 0:QK_COLS]
    XR_BANK, QT_BANK, KT_BANK, ON_BANK, WO_BANK = (0, 6), (0, 2), (6, 4), (0, 4), (2, 6)

    CHUNK = BANK
    def units(a):
        out = []
        for e in range(PAIR):
            for g in range(KV_HEADS):
                if a == 0:
                    for c in range(S // CHUNK):
                        for kt in range((c + 1) * CHUNK // P):
                            q0 = max(kt * P, c * CHUNK)
                            out.append((e, g, kt, q0, (c + 1) * CHUNK - q0, c))
                else:
                    for kt in range(TILES):
                        out.append((e, g, kt, kt * P, min(SPAN_A, S - kt * P), kt // 4))
        return out
    UNITS = [units(0), units(1)]
    STEPS = [2, 1]
    unit0 = [0, len(UNITS[0])]
    step0 = [0, STEPS[0] * len(UNITS[0])]
    n_chunks = PAIR * KV_HEADS * 2
    n_heads = PAIR * KV_HEADS
    steps_per_head = [STEPS[a] * len(UNITS[a]) // n_heads for a in range(2)]

    def is_masked(a, unit):
        return a == 1 or unit[3] == unit[2] * P

    masked_before = [[sum(is_masked(i, u) for i in range(a) for u in UNITS[i]) +
                      sum(is_masked(a, u) for u in UNITS[a][:n]) for n in range(len(UNITS[a]))]
                     for a in range(2)]

    def opens_bank(a, kt, ch, cc):
        return (kt == 0 and ch == cc) if a == 0 or cc == 0 else kt == 3

    DVE_HEADS = 3

    def mask_window(engine, n, h0, h1):
        width = UNITS[1][n][4]
        heads = probs[:, (unit0[1] + n) % E_BUFS, h0:h1, 0:width]
        return engine.tensor_tensor(heads, heads, widen(keep.local_mask[:, 0:1, 0:width], [P, h1 - h0, width]),
                                    ALU.mult)

    block = nc.Block()
    block.__enter__()

    @block.sync
    def _(sp):
        for e in range(PAIR):
            sp.dma_start(x[:, e], dram["hidden"][pair, e]).then_inc(x_loaded, 16)
        for n in range(2 * n_heads):
            a, e, g = n // n_heads, n % n_heads // KV_HEADS, n % KV_HEADS
            slot = n % 2
            if g == 0:
                sp.wait_ge(hi_ready, 2 * (PAIR * a + e + 1))
                sp.wait_ge(lo_ready, 2 * (PAIR * a + e + 1))
            if n >= 2:
                sp.wait_ge(scores_done, min(n - 1, n_heads) * steps_per_head[0] +
                           max(n - 1 - n_heads, 0) * steps_per_head[1])
            rows = slice(g * P // KV_HEADS, (g + 1) * P // KV_HEADS)
            for part, src in enumerate((q_hi, q_lo, q_hi, q_lo)):
                sp.dma_start(q_stack[part::PARTS, slot, :].bitcast(F32),
                             src[rows, e, :].bitcast(F32)).then_inc(gathered[slot], 16)
            for head in range(GROUP):
                sp.dma_start(k_stack[32 * head:32 * head + 32, slot, head, :].bitcast(F32),
                             k_parts[rows, e, :].bitcast(F32)).then_inc(gathered[slot], 16)

    PER_GATHER = 16 * (PARTS + GROUP)

    @block.gpsimd
    def _(pool):
        c = Chain(pool, pool_steps)
        for i in range(2 * PAIR):
            e = i % PAIR
            pool.wait_ge(qk_root_ready, i + 1)
            newton_step(pool, c, rnorm[:, e], refine[:, e], root[:, e], mean_sq[:, e], rnorm_ready)
        for n, (e, g, kt, q0, width, ch) in enumerate(UNITS[1]):
            pool.wait_ge(exp_done, step0[1] + (n + 1) * STEPS[1])
            mask_window(pool, n, DVE_HEADS, GROUP).then_inc(masked_rest, 1)

    @block.tensor
    def _(pe):
        T = nc.tensor
        for e in range(PAIR):
            pe.wait_ge(cond_rep_ready, e + 1)
            for i in range(2):
                ins = T.matmul(psum[:, (2 * e + i) * BANK:(2 * e + i) * BANK + 3 * D], cond_rep[:, e],
                               keep.wmod[:, i * 3 * D:(i + 1) * 3 * D], start=True, stop=True)
            ins.then_inc(mod_in_psum, 1)
        pe.wait_ge(mod_copied, PAIR)
        for a in range(2):
            for e in range(PAIR):
                pe.wait_ge(xr_ready, PAIR * a + e + 1)
                for t in range(TILES):
                    ins = T.transpose(psum[:, XR_BANK[e] * BANK + t * P:XR_BANK[e] * BANK + (t + 1) * P],
                                      nrm[:, e, t, :], keep.ident[:])
                    if t % 4 == 3:
                        ins.then_inc(xrt_in_psum, 1)
            for e in range(PAIR):
                if e == 1:
                    pe.wait_ge(v_ready, PAIR * a + 1)
                for t in range(TILES):
                    if t % 4 == 0:
                        pe.wait_ge(ht_ready, 2 * (PAIR * a + e) + t // 4 + 1)
                    ins = T.matmul(qkv_tiles[:, t, 0:QKV_COLS], ht[:, e, t * P:(t + 1) * P],
                                   keep.w_qkv[a][:], start=True, stop=True)
                ins.then_inc(qkv_in_psum, 1)
            for e in range(PAIR):
                pe.wait_ge(rot_ready, PAIR * a + e + 1)
                if e == 1:
                    pe.wait_ge(v_ready, PAIR * (a + 1))
                q0, k0 = QT_BANK[e] * BANK, KT_BANK[e] * BANK
                for t in range(TILES):
                    T.transpose(psum[:, q0 + t * P:q0 + (t + 1) * P], rot2[:, e, t, 0:P], keep.ident[:])
                for t in range(TILES):
                    ins = T.transpose(psum[:, k0 + t * P:k0 + (t + 1) * P], k_rep[:, e, t, :], keep.ident[:])
                ins.then_inc(qkt_in_psum, 1)
            pe.wait_ge(hi_ready, 2 * PAIR * (a + 1))
            pe.wait_ge(lo_ready, 2 * PAIR * (a + 1))

            def back_transpose(i):
                pe.wait_ge(ot_copied, i + 1)
                if i >= 2:
                    pe.wait_ge(o_ready, i - 1)
                cc = i % 2
                for t in range(4):
                    ins = T.transpose(psum[:, (6 + cc) * BANK + t * P:(6 + cc) * BANK + (t + 1) * P],
                                      o_t[:, cc * BANK + t * P:cc * BANK + (t + 1) * P], keep.ident[:])
                ins.then_inc(o_in_psum, 1)

            def values(n):
                e, g, kt, q0, width, ch = UNITS[a][n]
                pe.wait_ge(exp_done, step0[a] + (n + 1) * STEPS[a])
                if is_masked(a, UNITS[a][n]):
                    pe.wait_ge(masked, masked_before[a][n] + 1)
                if a == 1:
                    pe.wait_ge(masked_rest, n + 1)
                chunks_before = a * n_chunks + 2 * (e * KV_HEADS + g)
                for cc in range(2):
                    if opens_bank(a, kt, ch, cc) and chunks_before:
                        pe.wait_ge(ot_copied, chunks_before - 1 + cc)
                for cc in range(2):
                    lo, hi = max(q0, cc * BANK), min(q0 + width, (cc + 1) * BANK)
                    if lo >= hi:
                        continue
                    for head in range(GROUP):
                        ins = T.matmul(psum[32 * head:32 * head + V_PAD, (4 + cc) * BANK + lo - cc * BANK:
                                            (4 + cc) * BANK + hi - cc * BANK],
                                       v[:, e, kt, g * V_PAD:(g + 1) * V_PAD],
                                       probs[:, (unit0[a] + n) % E_BUFS, head, lo - q0:hi - q0],
                                       start=opens_bank(a, kt, ch, cc), stop=kt == 4 * cc + 3,
                                       skip_group_check=True)
                ins.then_inc(pv_done, 1)

            n_units = len(UNITS[a])
            pending = []
            done_chunks = a * n_chunks
            LAG = 2
            for n in range(n_units + LAG):
                if n < n_units:
                    e, g, kt, q0, width, ch = UNITS[a][n]
                    if kt == 0 and (a == 1 or ch == 0):
                        turn = a * n_heads + e * KV_HEADS + g
                        pe.wait_ge(gathered[turn % 2], PER_GATHER * (turn // 2 + 1))
                    for j in range(STEPS[a]):
                        step = step0[a] + n * STEPS[a] + j
                        if step >= 2:
                            pe.wait_ge(exp_done, step - 1)
                        heads = range(2 * j, 2 * j + 2) if a == 0 else range(GROUP)
                        for i, head in enumerate(heads):
                            base = (step % 2) * 2 * BANK + i * (BANK if a == 0 else BANK // 2)
                            w = width if a == 0 else min(192, S - q0)
                            ins = T.matmul(psum[:, base:base + w], k_stack[:, g % 2, head, kt * P:(kt + 1) * P],
                                           q_stack[:, g % 2, q0:q0 + w], start=True, stop=True)
                        ins.then_inc(scores_done, 1)
                if n >= LAG:
                    values(n - LAG)
                    kt, ch = UNITS[a][n - LAG][2], UNITS[a][n - LAG][5]
                    if pending and n - pending[0][1] >= 2:
                        back_transpose(pending.pop(0)[0])
                    if kt == 4 * ch + 3:
                        pending.append((done_chunks, n))
                        done_chunks += 1
            for i, _ in pending:
                back_transpose(i)
            for e in range(PAIR):
                pe.wait_ge(o_ready, a * n_chunks + (e + 1) * n_chunks // PAIR)
                if e == 0:
                    pe.wait_ge(exp_done, step0[a] + STEPS[a] * n_units)
                else:
                    pe.wait_ge(ot_copied, (a + 1) * n_chunks)
                for t in range(TILES):
                    ins = T.transpose(psum[:, ON_BANK[e] * BANK + t * P:ON_BANK[e] * BANK + (t + 1) * P],
                                      o[:, e, t, :], keep.ident[:])
                    if t % 4 == 3:
                        ins.then_inc(onT_in_psum, 1)
            for e in range(PAIR):
                for t in range(TILES):
                    if t % 4 == 0:
                        pe.wait_ge(onT_copied, 2 * (PAIR * a + e) + t // 4 + 1)
                    ins = T.matmul(psum[:, WO_BANK[e] * BANK + t * P:WO_BANK[e] * BANK + (t + 1) * P],
                                   ht[:, e, t * P:(t + 1) * P], keep.w_o[a][:], start=True, stop=True)
                ins.then_inc(wo_in_psum, 1)
        for e in range(PAIR):
            pe.wait_ge(n_ready, e + 1)
            for t in range(TILES):
                ins = T.transpose(psum[:, ON_BANK[e] * BANK + t * P:ON_BANK[e] * BANK + (t + 1) * P],
                                  nrm[:, e, t, :], keep.ident[:])
            ins.then_inc(nt_in_psum, 1)

    @block.scalar
    def _(act):
        c = Chain(act, act_steps)
        act.preload_act_table_set(ROOTS_AND_EXP)
        silu = keep.silu[:].rearrange("p (q e) -> p q e", e=PAIR)[:, pair]
        for e in range(PAIR):
            act.activation(cond_rep[:, e], widen(silu[:, e:e + 1], [P, P]), ACT.Copy).then_inc(cond_rep_ready, 1)
        for e in range(PAIR):
            act.wait_ge(mod_in_psum, e + 1)
            for i in range(2):
                src = psum[:, (2 * e + i) * BANK:(2 * e + i) * BANK + 3 * D]
                c.did(act.activation(mod[:, e, i * 3 * D:(i + 1) * 3 * D], src, ACT.Copy),
                      mod_copied if i else None)

        def inverse_root(out, in_, signal):
            c.did(act.activation(out, in_, ACT.Ln))
            c.settle()
            c.did(act.activation(out, out, ACT.Exp, scale=-0.5), signal)

        def row_roots(turn):
            for e in range(PAIR):
                act.wait_ge(row_sq_ready, PAIR * turn + e + 1)
                inverse_root(row_root[:, e], row_sq[:, e], row_root_ready)

        row_roots(0)
        for a in range(2):
            for e in range(PAIR):
                act.wait_ge(h_ready, PAIR * a + e + 1)
                c.did(act.activation(nrm[:, e], h[:, e], ACT.Square), sq_ready)
            row_roots(a + 1)
            for e in range(PAIR):
                for i in range(2):
                    n = XR_BANK[e] + i
                    act.wait_ge(xrt_in_psum, 2 * (PAIR * a + e) + i + 1)
                    c.did(act.activation(ht[:, e, i * BANK:(i + 1) * BANK], psum[:, n * BANK:(n + 1) * BANK],
                                         ACT.Copy, scale=keep.norm_w[:, a:a + 1]), ht_ready)
            for e in range(PAIR):
                act.wait_ge(qkv_in_psum, PAIR * a + e + 1)
                c.did(act.activation(qk[:, e], qk_ps, ACT.Copy), qk_copied)
                c.did(act.activation(v4[:, e, :, :, 0:HEAD_DIM],
                                     qkv_tiles[:, :, QK_COLS:QKV_COLS].rearrange("p t (g d) -> p t g d", g=KV_HEADS),
                                     ACT.Copy), v_ready)
                act.wait_ge(qk_copied, PAIR * a + e + 1)
                c.did(act.activation(rot2[:, e], qk[:, e], ACT.Square), qk_sq_ready)
            for e in range(PAIR):
                act.wait_ge(mean_sq_ready, PAIR * a + e + 1)
                inverse_root(root[:, e], mean_sq[:, e], qk_root_ready)
            for e in range(PAIR):
                act.wait_ge(qkt_in_psum, PAIR * a + e + 1)
                c.did(act.activation(k_parts[:, e, :], ps2(KT_BANK[e]), ACT.Copy, scale=keep.part[:, 0:1]),
                      hi_ready)
                c.did(act.activation(q_hi[:, e], ps2(QT_BANK[e]), ACT.Copy), hi_ready)
            for n, (e, g, kt, q0, width, ch) in enumerate(UNITS[a]):
                for j in range(STEPS[a]):
                    step = step0[a] + n * STEPS[a] + j
                    act.wait_ge(scores_done, step + 1)
                    if unit0[a] + n >= E_BUFS and j == 0:
                        act.wait_ge(pv_done, unit0[a] + n - E_BUFS + 1)
                    buf = probs[:, (unit0[a] + n) % E_BUFS, :, :]
                    src = ps2((step % 2) * 2)
                    if a == 0:
                        dst, src = buf[:, 2 * j:2 * j + 2, 0:width], src.rearrange("p (h c) -> p h c", h=2)
                    else:
                        dst, src = buf[:, :, 0:width], src.rearrange("p (h c) -> p h c", h=GROUP)
                    act.activation(dst, src[:, :, 0:width], ACT.Exp,
                                   scale=float(1.0 / np.sqrt(np.float32(HEAD_DIM)))).then_inc(exp_done, 1)
            for e in range(PAIR):
                for i in range(2):
                    n = ON_BANK[e] + i
                    act.wait_ge(onT_in_psum, 2 * (PAIR * a + e) + i + 1)
                    c.did(act.activation(ht[:, e, i * BANK:(i + 1) * BANK], psum[:, n * BANK:(n + 1) * BANK],
                                         ACT.Copy), onT_copied)
        row_roots(3)
        for e in range(PAIR):
            act.wait_ge(nt_in_psum, e + 1)
            for half, shift in ((slice(0, 64), 0), (slice(64, P), 1)):
                c.did(act.activation(state[half, e, shift:shift + S],
                                     psum[half, ON_BANK[e] * BANK:ON_BANK[e] * BANK + S], ACT.Copy))
        c.settle()

    @block.vector
    def _(dve):
        c = Chain(dve, dve_steps)
        V = nc.vector
        dve.wait_ge(mod_copied, PAIR)
        m6 = mod[:].rearrange("p e (i j d) -> p e i j d", i=2, j=3)
        scales, gates = m6[:, :, :, 1, :], m6[:, :, :, 2, :]
        c.did(V.tensor_scalar(scales, scales, 1.0, None, ALU.add))
        c.did(V.tensor_scalar(gate_tmp[:], gates, 0.0, 2.0, ALU.is_ge, ALU.mult))
        c.settle()
        for turn in range(2):
            c.did(V.scalar_tensor_tensor(gates, gate_tmp[:], -1.0, gates, ALU.add, ALU.mult))
            c.settle()
            if turn == 0:
                c.did(V.tensor_scalar(gates, gates, 0.25, None, ALU.max))
                c.settle()
        c.did(V.tensor_copy(gate_b, mod[:, :, 5 * D:6 * D]))
        row = lambda e, i: widen(mod[:, e, i * D:(i + 1) * D].rearrange("p (o d) -> p o d", o=1), [P, TILES, D])

        def refine_root(e):
            newton_step(dve, c, rstd[:, e], row_refine[:, e], row_root[:, e], row_sq[:, e], None)
            c.settle()

        def layernorms(dst, turn, scale_row, shift_row, signal):
            for e in range(PAIR):
                for t in range(TILES):
                    c.did(V.bn_stats(stats[:, e, t, :], x[:, e, t, :]))
                c.settle()
                for t in range(TILES):
                    c.did(V.bn_aggr(mv[:, e, t, :], stats[:, e, t, :]))
                c.settle()
                c.did(V.tensor_scalar(row_sq[:, e], mv[:, e, :, 1], LN_EPS, None, ALU.add), row_sq_ready)
            for e in range(PAIR):
                dve.wait_ge(row_root_ready, PAIR * turn + e + 1)
                refine_root(e)
                for t in range(TILES):
                    c.did(V.tensor_scalar(dst[:, e, t, :], x[:, e, t, :], mv[:, e, t, 0:1], rstd[:, e, t:t + 1],
                                          ALU.subtract, ALU.mult))
                c.settle()
                c.did(V.tensor_tensor(dst[:, e], dst[:, e], row(e, scale_row), ALU.mult))
                c.settle()
                c.did(V.tensor_tensor(dst[:, e], dst[:, e], row(e, shift_row), ALU.add), signal)

        dve.wait_ge(x_loaded, 16 * PAIR)
        layernorms(h, 0, 1, 0, h_ready)
        for a in range(2):
            for e in range(PAIR):
                dve.wait_ge(sq_ready, PAIR * a + e + 1)
                c.did(V.tensor_reduce(row_sq[:, e], nrm[:, e], AX, ALU.add))
                c.settle()
                c.did(V.tensor_scalar(row_sq[:, e], row_sq[:, e], 1.0 / D, ATT_EPS, ALU.mult, ALU.add),
                      row_sq_ready)
            for e in range(PAIR):
                dve.wait_ge(row_root_ready, PAIR * (a + 1) + e + 1)
                refine_root(e)
                c.did(V.tensor_tensor(nrm[:, e], h[:, e],
                                      widen(rstd[:, e].rearrange("p (t o) -> p t o", o=1), [P, TILES, D]),
                                      ALU.mult), xr_ready)
            by_dim = lambda ap: ap.rearrange("p t (d h) -> p t d h", h=QK_HEADS)
            cos_sin = keep.rope_a[:, a, :, :, :]
            cos = cos_sin[:, 0, :, :].rearrange("p t (d o) -> p t d o", o=1)
            sin = cos_sin[:, 1, :, :].rearrange("p t (d o) -> p t d o", o=1)
            for e in range(PAIR):
                i = PAIR * a + e
                dve.wait_ge(qk_copied, i + 1)
                c.did(V.tensor_tensor(by_dim(rot[:, e]), by_dim(qk[:, e]),
                                      widen(cos, [P, TILES, HEAD_DIM, QK_HEADS]), ALU.mult))
                dve.wait_ge(qk_sq_ready, i + 1)
                c.did(V.tensor_reduce(mean_sq[:, e], rot2[:, e].rearrange("p t (d h) -> p t h d", h=QK_HEADS),
                                      AX, ALU.add))
                c.settle()
                c.did(V.tensor_scalar(mean_sq[:, e], mean_sq[:, e], 1.0 / HEAD_DIM, ATT_EPS, ALU.mult, ALU.add),
                      mean_sq_ready)
                for half in range(2):
                    d0, d1 = half * PAIRS, (1 - half) * PAIRS
                    c.did(V.tensor_tensor(by_dim(rot2[:, e])[:, :, d0:d0 + PAIRS, :],
                                          by_dim(qk[:, e])[:, :, d1:d1 + PAIRS, :],
                                          widen(sin[:, :, d0:d0 + PAIRS, :], [P, TILES, PAIRS, QK_HEADS]), ALU.mult))
                c.settle()
                c.did(V.tensor_tensor(rot[:, e], rot[:, e], rot2[:, e], ALU.add))
                dve.wait_ge(rnorm_ready, i + 1)
                c.settle()
                rn = rnorm[:, e].rearrange("p t (o h) -> p t o h", o=1)
                rows = by_dim(rot[:, e])
                c.did(V.tensor_tensor(rot2[:, e, :, 0:P].rearrange("p t (h d) -> p t d h", h=HEADS),
                                      rows[:, :, :, 0:HEADS],
                                      widen(rn[:, :, :, 0:HEADS], [P, TILES, HEAD_DIM, HEADS]), ALU.mult))
                for g in range(KV_HEADS):
                    col = HEADS + g
                    c.did(V.tensor_tensor(
                        k_rep[:, e, :, 32 * g:32 * (g + 1)].rearrange("p t (d r) -> p t d r", r=PARTS),
                        widen(rows[:, :, :, col:col + 1], [P, TILES, HEAD_DIM, PARTS]),
                        widen(rn[:, :, :, col:col + 1], [P, TILES, HEAD_DIM, PARTS]), ALU.mult),
                        rot_ready if g == KV_HEADS - 1 else None)
            for e in range(PAIR):
                i = PAIR * a + e
                dve.wait_ge(hi_ready, 2 * i + 1)
                c.did(V.scalar_tensor_tensor(k_parts[:, e, :], ps2(KT_BANK[e]), keep.part[:, 1:2],
                                             k_parts[:, e, :].bitcast(F32), ALU.mult, ALU.add), lo_ready)
                dve.wait_ge(hi_ready, 2 * i + 2)
                c.did(V.tensor_tensor(q_lo[:, e], ps2(QT_BANK[e]), q_hi[:, e].bitcast(F32), ALU.subtract), lo_ready)

            pending, to_copy = [], []
            chunks = a * n_chunks

            def copy_chunk(i, n):
                ch = i % 2
                dve.wait_ge(pv_done, unit0[a] + n + 1)
                if i >= 2:
                    dve.wait_ge(o_in_psum, i - 1)
                c.did(V.tensor_copy(o_t[:, ch * BANK:(ch + 1) * BANK],
                                    psum[:, (4 + ch) * BANK:(5 + ch) * BANK]), ot_copied)

            def normalise(i):
                e, r = divmod(i - a * n_chunks, n_chunks // PAIR)
                g, cc = r // 2, r % 2
                dve.wait_ge(o_in_psum, i + 1)
                src = psum[:, (6 + cc) * BANK:(7 + cc) * BANK].rearrange("p (t h c) -> p t h c", t=4, h=GROUP)
                c.settle()
                c.did(V.reciprocal(o_rec[:], src[:, :, :, HEAD_DIM]))
                c.settle()
                dst = o[:, e, 4 * cc:4 * cc + 4, g * GROUP * HEAD_DIM:(g + 1) * GROUP * HEAD_DIM]
                c.did(V.tensor_tensor(dst.rearrange("p t (h d) -> p t h d", h=GROUP), src[:, :, :, 0:HEAD_DIM],
                                      widen(o_rec[:].rearrange("p t (h o) -> p t h o", o=1),
                                            [P, 4, GROUP, HEAD_DIM]), ALU.mult), o_ready)

            for n, (e, g, kt, q0, width, ch) in enumerate(UNITS[a]):
                buf = probs[:, (unit0[a] + n) % E_BUFS, :, :]
                if is_masked(a, UNITS[a][n]):
                    dve.wait_ge(exp_done, step0[a] + (n + 1) * STEPS[a])
                    if a == 1:
                        c.did(mask_window(V, n, 0, DVE_HEADS), masked)
                    else:
                        c.did(V.tensor_tensor(buf[:, :, 0:P], buf[:, :, 0:P],
                                              widen(keep.causal_mask[:], [P, GROUP, P]), ALU.mult), masked)
                if to_copy and n - to_copy[0][1] >= 2:
                    copy_chunk(*to_copy.pop(0))
                if pending and n - pending[0][1] >= 5:
                    normalise(pending.pop(0)[0])
                if kt == 4 * ch + 3:
                    to_copy.append((chunks, n))
                    pending.append((chunks, n))
                    chunks += 1
            for i, n in to_copy:
                copy_chunk(i, n)
            for i, _ in pending:
                normalise(i)
            for e in range(PAIR):
                dve.wait_ge(wo_in_psum, PAIR * a + e + 1)
                c.did(V.tensor_tensor(h[:, e], h[:, e], ps2(WO_BANK[e]).rearrange("p (t d) -> p t d", t=TILES),
                                      ALU.add), h_ready)
        for e in range(PAIR):
            c.settle()
            c.did(V.tensor_tensor(h[:, e], h[:, e], row(e, 2), ALU.mult))
            c.settle()
            c.did(V.tensor_tensor(x[:, e], x[:, e], h[:, e], ALU.add))
        c.settle()
        layernorms(nrm, 3, 4, 3, n_ready)
        c.settle()

    block.__exit__(None, None, None)
    k.clear_semaphores()


def attention_half(nc, psum, dram, keep):
    with Scope(nc, "att") as k:
        k.k_stack = k.sb("k_stack", [P, 2, GROUP, S], F32R)
        k.v = k.sb("v", [P, PAIR, TILES, KV_HEADS * V_PAD])
        zeroed = k.sem("zeroed")
        with nc.Block() as block:
            @block.gpsimd
            def _(pool):
                pool.memset(k.k_stack[:].bitcast(F32), 0.0)
                pool.memset(k.v[:], 0.0).then_inc(zeroed, 1)
                pool.wait_ge(zeroed, 1)
                v4 = k.v[:].rearrange("p e t (g c) -> p e t g c", g=KV_HEADS)
                pool.memset(v4[:, :, :, :, HEAD_DIM:HEAD_DIM + 1], 1.0)
        k.clear_semaphores()
        with nc.Fori(0, B // PAIR) as pair:
            attention_pair(nc, psum, dram, keep, k, pair)


class Kept:
    pass


def keep_tensors(nc, stack):
    keep = Kept()
    sb = lambda n, shape, dt=F32: stack.enter_context(nc.sbuf_tensor(n, shape, dt))
    keep.ident, keep.ident_bf = sb("ident", [P, P]), sb("ident_bf", [P, P], BF16)
    keep.eps = sb("epsilons", [P, 3])
    keep.part = sb("part", [P, 2])
    keep.wmod = sb("wmod", [P, 6 * D])
    keep.w_qkv = [sb(f"w_qkv{a}", [P, QKV_COLS]) for a in range(2)]
    keep.w_o = [sb(f"w_o{a}", [P, D]) for a in range(2)]
    keep.norm_w = sb("norm_w", [P, 2])
    keep.rope_a = sb("rope_a", [P, 2, 2, TILES, HEAD_DIM])
    keep.local_mask, keep.causal_mask = sb("local_mask", [P, 1, SPAN_A]), sb("causal_mask", [P, 1, P])
    keep.silu = sb("silu", [D, B])
    keep.gate_b = sb("gate_b", [P, B, D])
    keep.xres = sb("xres", [P, B, TILES, D])
    keep.xs = sb("xs", [P, B, S + 2])
    return keep

def load_layer(nc, dram, k, layer):
    loads = [
        (k.w_qkv[:], dram["f_wqkv"][layer]), (k.w_o[:], dram["f_wo"][layer]),
        (k.w1[:], dram["f_w1"][layer]), (k.w2[:], dram["f_w2"][layer]),
        (k.vec[:], dram["f_vec"][layer]), (k.b1[:], dram["f_b1"][layer]),
        (k.qk_scale[:], dram["f_scale"][layer]),
    ]
    loaded, tables = k.layer_loaded, k.tables_done
    with nc.Block() as block:
        @block.sync
        def _(sp):
            for dst, src in loads:
                sp.dma_start(dst, src).then_inc(loaded, 16)

        @block.vector
        def _(dve):
            dve.wait_ge(loaded, 16 * len(loads))
            h = FD // 2
            base_sin, sin = (tab[:].rearrange("p t (i d) -> p t i d", i=2) for tab in (k.base_sin, k.sin))
            scale = k.qk_scale[:].rearrange("p (o i d) -> p o i d", o=1, i=2)
            nc.vector.tensor_tensor(k.cos[:], k.base_cos[:],
                                    widen(k.qk_scale[:].rearrange("p (o d) -> p o d", o=1), [P, TILES, 2 * FD]),
                                    ALU.mult).then_inc(tables, 1)
            for lo in (0, h):
                other = h - lo
                nc.vector.tensor_tensor(sin[:, :, :, lo:lo + h], base_sin[:, :, :, lo:lo + h],
                                        widen(scale[:, :, :, other:other + h], [P, TILES, 2, h]),
                                        ALU.mult).then_inc(tables, 1)
    with nc.Block() as block:
        @block.sync
        def _(sp):
            sp.sem_clear(loaded)
            sp.sem_clear(tables)


FFN_SIGNALS = """xw_ready qk_in_psum v_in_psum sq_ready ssq_ready v_copied root_ready rn_ready roped added qk_rotated k_rotated
    qkt_in_psum qkt_copied s_in_psum maxed neg_ready mt_in_psum mt_copied st_in_psum exped
    o_in_psum o_normed ot_in_psum ot_copied wo_in_psum resid_done xt_in_psum mv_ready rstd_ready
    xn_ready hn_in_psum hn_ready ag_in_psum gelu_ready u_ready y_in_psum
    act_steps dve_steps pool_steps""".split()


DVE_NORM = 10


def scale_heads(engine, chain, k, t, h0, h1, signal):
    r = k.rot[:, t % 2, h0 * FD:h1 * FD].rearrange("p (h d) -> p h d", d=FD)
    rn = k.rnorm[:, t % 2, h0:h1].rearrange("p (h o) -> p h o", o=1)
    chain.did(engine.tensor_tensor(r, r, widen(rn, [P, h1 - h0, FD]), ALU.mult), signal)


def ffn_batch(nc, psum, keep, k, b):
    g = k.signals
    bank = lambda i, n=1: psum[:, i * BANK:(i + n) * BANK]
    HN_BANK, Y_BANK = (3, 6), (4, 5)
    slot = BANK // 2

    def score_cols(t):
        return (WIN if t == 0 else 0), SPAN_F

    def st_width(kt):
        return min(SPAN_F, S - kt * P)

    block = nc.Block()
    block.__enter__()

    @block.tensor
    def _(pe):
        T = nc.tensor
        pe.wait_ge(g["xw_ready"], 1)
        def project(t):
            x_t = k.xw[:, t * P:(t + 1) * P]
            if t >= 2:
                pe.wait_ge(g["roped"], t - 1)
            for i in range(2):
                ins = T.matmul(bank(2 * (t % 2) + i), x_t, k.w_qkv[:, i * INNER:(i + 1) * INNER],
                               start=True, stop=True)
            ins.then_inc(g["qk_in_psum"], 1)
            if t >= 2:
                pe.wait_ge(g["v_copied"], t - 1)
            T.matmul(bank(4 + t % 2), x_t, k.w_qkv[:, 2 * INNER:3 * INNER],
                     start=True, stop=True).then_inc(g["v_in_psum"], 1)

        def qk_transposes(t):
            pe.wait_ge(g["qk_rotated"], t + 1)
            pe.wait_ge(g["k_rotated"], t + 1)
            if t >= 1:
                pe.wait_ge(g["qkt_copied"], t)
            for i in range(8):
                ins = T.transpose(psum[:, 6 * BANK + i * P:6 * BANK + (i + 1) * P],
                                  k.rot[:, t % 2, i * P:(i + 1) * P], keep.ident[:])
            ins.then_inc(g["qkt_in_psum"], 1)

        LAG1 = 2
        for t in range(TILES):
            project(t)
            if t >= LAG1:
                qk_transposes(t - LAG1)

        pe.wait_ge(g["roped"], TILES)
        pe.wait_ge(g["v_copied"], TILES)

        def query_scores(t):
            lo, hi = score_cols(t)
            key0 = t * P - WIN
            pe.wait_ge(g["qkt_copied"], t + 1)
            for hf in range(2):
                if t >= 1:
                    pe.wait_ge(g["maxed"], 2 * t + hf - 1)
                for i in range(4):
                    head = 4 * hf + i
                    out = psum[:, 2 * hf * BANK + i * slot + lo:2 * hf * BANK + i * slot + hi]
                    T.matmul(out, k.q_t_bf[:, head // 2, t * P:(t + 1) * P, 1],
                             k.k_t_bf[:, head, key0 + lo:key0 + hi, 1], start=True, stop=False)
                    ins = T.matmul(out, keep.ident_bf[:], k.band_bf[:, lo:hi], start=False, stop=True)
                ins.then_inc(g["s_in_psum"], 1)

        def max_transpose(t):
            pe.wait_ge(g["neg_ready"], t + 1)
            if t >= 2:
                pe.wait_ge(g["mt_copied"], t - 1)
            T.transpose(bank(4 + t % 2).bitcast(BF16)[0:FH, 0:P], k.neg_max[:, t, :],
                        keep.ident_bf[:]).then_inc(g["mt_in_psum"], 1)

        for t in range(TILES + 1):
            if t < TILES:
                query_scores(t)
            if t < LAG1:
                qk_transposes(TILES - LAG1 + t)
            if t >= 1:
                max_transpose(t - 1)

        pe.wait_ge(g["maxed"], 2 * TILES)

        def key_scores(kt, hf):
            w = st_width(kt)
            pe.wait_ge(g["mt_copied"], min(kt + 2, TILES))
            if kt >= 1:
                pe.wait_ge(g["exped"], 2 * kt + hf - 1)
            for i in range(4):
                head = 4 * hf + i
                out = psum[:, 2 * hf * BANK + i * slot:2 * hf * BANK + i * slot + w]
                T.matmul(out, k.k_t[:, head, kt * P:(kt + 1) * P], k.q_t[:, head // 2, kt * P:kt * P + w],
                         start=True, stop=False)
                T.matmul(out, k.pick[:, head, :], k.max_t[:, kt * P:kt * P + w], start=False, stop=False)
                ins = T.matmul(out, keep.ident_bf[:], k.band_t_bf[:, 0:w], start=False, stop=True)
            ins.then_inc(g["st_in_psum"], 1)

        def value_products(t):
            for hf in range(2):
                pe.wait_ge(g["exped"], 2 * t + hf + 1)
                if t >= 1:
                    pe.wait_ge(g["o_normed"], 2 * t + hf - 1)
                for i in range(4):
                    head = 4 * hf + i
                    v0 = head * VF_STRIDE
                    c0 = (4 + hf) * BANK + i * VF_STRIDE
                    ins = T.matmul(psum[:, c0:c0 + VF_MOVE], k.probs[:, t % 3, head, 0:P],
                                   k.v[:, t, v0:v0 + VF_MOVE], start=True, stop=True)
                    if t >= 1:
                        ins = T.matmul(psum[0:WIN, c0:c0 + VF_MOVE], k.probs[:, (t - 1) % 3, head, P:SPAN_F],
                                       k.v[:, t - 1, v0:v0 + VF_MOVE], start=False, stop=True,
                                       skip_group_check=True)
                ins.then_inc(g["o_in_psum"], 1)

        def out_transposes(t):
            pe.wait_ge(g["o_normed"], 2 * t + 2)
            if t >= 1:
                pe.wait_ge(g["ot_copied"], t)
            for i in range(4):
                ins = T.transpose(psum[:, 6 * BANK + i * P:6 * BANK + (i + 1) * P],
                                  k.o[:, t % 2, i * P:(i + 1) * P], keep.ident[:])
            ins.then_inc(g["ot_in_psum"], 1)

        def project_out(c):
            pe.wait_ge(g["ot_copied"], 4 * c + 4)
            if c >= 1:
                pe.wait_ge(g["resid_done"], c)
                pe.wait_ge(g["xn_ready"], c)
            for i in range(4):
                ins = T.matmul(bank(7), k.w_o[:, i, :], k.o_t[:, i, :], start=i == 0, stop=i == 3)
            ins.then_inc(g["wo_in_psum"], 1)

        def x_transposes(c):
            pe.wait_ge(g["resid_done"], c + 1)
            for i in range(4):
                t = 4 * c + i
                ins = T.transpose(psum[:, 7 * BANK + i * P:7 * BANK + (i + 1) * P],
                                  k.xw[:, t * P:(t + 1) * P], keep.ident[:])
            ins.then_inc(g["xt_in_psum"], 1)

        def xn_transposes(c):
            pe.wait_ge(g["xn_ready"], c + 1)
            if c == 0:
                pe.wait_ge(g["exped"], 2 * TILES)
            else:
                pe.wait_ge(g["ot_copied"], TILES)
            for i in range(4):
                ins = T.transpose(psum[:, HN_BANK[c] * BANK + i * P:HN_BANK[c] * BANK + (i + 1) * P],
                                  k.xn[:, 4 * c + i, :], keep.ident[:])
            ins.then_inc(g["hn_in_psum"], 1)

        def up(n):
            c, j = divmod(n, 3)
            pe.wait_ge(g["hn_ready"], c + 1)
            if n >= 2:
                pe.wait_ge(g["u_ready"], n - 1)
            r0, rows = HID_BLOCKS[j]
            for i in range(2):
                ins = T.matmul(psum[0:rows, (2 * (n % 2) + i) * BANK:(2 * (n % 2) + i + 1) * BANK],
                               k.w1[:, i * HID + r0:i * HID + r0 + rows],
                               k.hn[:, c * BANK:(c + 1) * BANK], start=True, stop=True)
            ins.then_inc(g["ag_in_psum"], 1)

        def down(c):
            pe.wait_ge(g["u_ready"], 3 * c + 3)
            for j, (r0, rows) in enumerate(HID_BLOCKS):
                ins = T.matmul(bank(Y_BANK[c]), k.w2[0:rows, j, :], k.u[0:rows, c, j, :],
                               start=j == 0, stop=j == 2)
            ins.then_inc(g["y_in_psum"], 1)

        for kt in range(TILES + 2):
            if kt < TILES:
                key_scores(kt, 0)
                key_scores(kt, 1)
            if 1 <= kt <= TILES:
                value_products(kt - 1)
            if kt >= 2:
                out_transposes(kt - 2)
            if kt == 6:
                project_out(0)
            if kt == 7:
                x_transposes(0)
        xn_transposes(0)
        project_out(1)
        up(0)
        up(1)
        x_transposes(1)
        up(2)
        xn_transposes(1)
        down(0)
        up(3)
        up(4)
        up(5)
        down(1)

    @block.scalar
    def _(act):
        c = Chain(act, g["act_steps"])
        act.preload_act_table_set(ROOTS_AND_EXP)

        def rotary_step(t):
            act.wait_ge(g["qk_in_psum"], t + 1)
            if t >= 1:
                act.wait_ge(g["ssq_ready"], t)
            c.did(act.activation(k.sq[:], bank(2 * (t % 2), 2), ACT.Square), g["sq_ready"])
            act.wait_ge(g["v_in_psum"], t + 1)
            v_t = k.v[:, t, 0:FH * VF_STRIDE].rearrange("p (h c) -> p h c", h=FH)
            c.did(act.activation(v_t[:, :, 0:FD], bank(4 + t % 2).rearrange("p (h d) -> p h d", h=FH),
                                 ACT.Copy), g["v_copied"])
            act.wait_ge(g["ssq_ready"], t + 1)
            if t >= 2:
                act.wait_ge(g["rn_ready"], t - 1)
            rn = k.root[:, t % 2, :]
            c.did(act.activation(rn, k.ssq[:, t % 2, :], ACT.Ln, scale=float(2 ** 20)))
            c.settle()
            c.did(act.activation(rn, rn, ACT.Exp, scale=-0.5, bias=keep.eps[:, 2:3]), g["root_ready"])

        def copy_qkt(t):
            act.wait_ge(g["qkt_in_psum"], t + 1)
            cols = slice(t * P, (t + 1) * P)
            c.did(act.activation(k.q_t[:, :, cols], bank(6).rearrange("p (i t) -> p i t", i=4), ACT.Copy))
            for j, half in ((0, slice(0, FD)), (1, slice(FD, P))):
                dst = k.k_t[half, :, cols].rearrange("p (i j) t -> p i j t", j=2)[:, :, j, :]
                c.did(act.activation(dst, psum[half, 7 * BANK:8 * BANK].rearrange("p (i t) -> p i t", i=4),
                                     ACT.Copy), g["qkt_copied"] if j else None)

        for t in range(TILES + 2):
            if t < TILES:
                rotary_step(t)
            if t >= 2:
                copy_qkt(t - 2)
        for t in range(TILES):
            act.wait_ge(g["mt_in_psum"], t + 1)
            c.did(act.activation(k.max_t[0:FH, t * P:(t + 1) * P],
                                 bank(4 + t % 2).bitcast(BF16)[0:FH, 0:P], ACT.Copy), g["mt_copied"])
        def row_roots(i):
            act.wait_ge(g["mv_ready"], i + 1)
            r = k.rstd[:, 4 * i:4 * i + 4, :]
            c.did(act.activation(r, k.mv[:, 4 * i:4 * i + 4, 1:2], ACT.Ln, bias=keep.eps[:, 0:1]))
            c.settle()
            c.did(act.activation(r, r, ACT.Exp, scale=-0.5), g["rstd_ready"])

        def hn_copy(i):
            act.wait_ge(g["hn_in_psum"], i + 1)
            c.did(act.activation(k.hn[:, i * BANK:(i + 1) * BANK], bank(HN_BANK[i]), ACT.Identity,
                                 scale=k.vec[:, 0:1], bias=k.vec[:, 1:2]), g["hn_ready"])

        for kt in range(TILES + 2):
            if kt < TILES:
                w = st_width(kt)
                for hf in range(2):
                    act.wait_ge(g["st_in_psum"], 2 * kt + hf + 1)
                    if kt >= 3:
                        act.wait_ge(g["o_in_psum"], 2 * (kt - 1))
                    src = bank(2 * hf, 2).rearrange("p (h c) -> p h c", h=4)
                    c.did(act.activation(k.probs[:, kt % 3, 4 * hf:4 * hf + 4, 0:w], src[:, :, 0:w], ACT.Exp,
                                         scale=QK_SCALE), g["exped"])
            if kt >= 2:
                t = kt - 2
                act.wait_ge(g["ot_in_psum"], t + 1)
                if t == 4:
                    act.wait_ge(g["wo_in_psum"], 1)
                c.did(act.activation(k.o_t[:, :, (t % 4) * P:(t % 4 + 1) * P],
                                     bank(6).rearrange("p (i t) -> p i t", i=4), ACT.Copy), g["ot_copied"])
            if kt == 8:
                row_roots(0)
        def gelu(n):
            j = n % 3
            rows = HID_BLOCKS[j][1]
            act.wait_ge(g["ag_in_psum"], n + 1)
            if n >= 2:
                act.wait_ge(g["u_ready"], n - 1)
            c.did(act.activation(k.gelu[0:rows, n % 2, :],
                                 psum[0:rows, (1 + 2 * (n % 2)) * BANK:(2 + 2 * (n % 2)) * BANK],
                                 ACT.Gelu, bias=k.b1[0:rows, 3 + j:4 + j]), g["gelu_ready"])

        hn_copy(0)
        gelu(0)
        gelu(1)
        act.preload_act_table_set(ROOTS_AND_EXP)
        row_roots(1)
        gelu(2)
        hn_copy(1)
        gelu(3)
        gelu(4)
        gelu(5)

    @block.gpsimd
    def _(pool):
        c = Chain(pool, g["pool_steps"])
        for t in range(TILES):
            pool.wait_ge(g["roped"], t + 1)
            c.did(pool.tensor_tensor(k.rot[:, t % 2, :], k.rot[:, t % 2, :], k.rot_sin[:, t % 2, :], ALU.add),
                  g["added"])
            pool.wait_ge(g["root_ready"], t + 1)
            if t >= 2:
                pool.wait_ge(g["qk_rotated"], t - 1)
            newton_step(pool, c, k.rnorm[:, t % 2, :], k.refine[:, t % 2, :], k.root[:, t % 2, :],
                        k.ssq[:, t % 2, :], g["rn_ready"])
            c.settle()
            scale_heads(pool, c, k, t, DVE_NORM, 2 * FH, g["k_rotated"])

    @block.vector
    def _(dve):
        c = Chain(dve, g["dve_steps"])
        V = nc.vector
        c.did(V.tensor_copy(k.xw[:, 0:S + 1], keep.xs[:, b, 0:S + 1]), g["xw_ready"])

        def rope(t):
            dve.wait_ge(g["sq_ready"], t + 1)
            if t >= 2:
                dve.wait_ge(g["rn_ready"], t - 1)
            c.did(V.tensor_reduce(k.ssq[:, t % 2, :], k.sq[:].rearrange("p (h d) -> p h d", d=FD), AX, ALU.add))
            c.settle()
            c.did(V.tensor_scalar(k.ssq[:, t % 2, :], k.ssq[:, t % 2, :], 1e-24, None, ALU.max), g["ssq_ready"])
            if t >= 2:
                dve.wait_ge(g["qkt_in_psum"], t - 1)
            src = bank(2 * (t % 2), 2).rearrange("p (i h d) -> p i h d", i=2, h=FH)
            heads = lambda tab: tab.rearrange("p (i o d) -> p i o d", i=2, o=1)
            as_heads = lambda ap: ap.rearrange("p (i h d) -> p i h d", i=2, h=FH)
            c.did(V.tensor_tensor(as_heads(k.rot[:, t % 2, :]), src,
                                  widen(heads(k.cos[:, t, :]), [P, 2, FH, FD]), ALU.mult))
            for lo in (0, FD // 2):
                other = FD // 2 - lo
                c.did(V.tensor_tensor(as_heads(k.rot_sin[:, t % 2, :])[:, :, :, lo:lo + FD // 2],
                                      src[:, :, :, other:other + FD // 2],
                                      widen(heads(k.sin[:, t, :])[:, :, :, lo:lo + FD // 2],
                                            [P, 2, FH, FD // 2]), ALU.mult), g["roped"] if lo else None)

        def normalise(t):
            dve.wait_ge(g["added"], t + 1)
            dve.wait_ge(g["rn_ready"], t + 1)
            scale_heads(V, c, k, t, 0, DVE_NORM, g["qk_rotated"])

        def row_maxima(t):
            lo, hi = score_cols(t)
            for hf in range(2):
                dve.wait_ge(g["s_in_psum"], 2 * t + hf + 1)
                src = bank(2 * hf, 2).rearrange("p (h c) -> p h c", h=4)
                c.did(V.tensor_reduce(k.row_max[:, t, 4 * hf:4 * hf + 4], src[:, :, lo:hi], AX, ALU.max),
                      g["maxed"])
            c.settle()
            c.did(V.tensor_scalar(k.neg_max[:, t, :], k.row_max[:, t, :], -1.0, None, ALU.mult), g["neg_ready"])

        for t in range(TILES):
            rope(t)
            if t >= 1:
                normalise(t - 1)
        row_maxima(0)
        normalise(TILES - 1)
        for t in range(1, TILES):
            row_maxima(t)

        def norm_out(t):
            for hf in range(2):
                dve.wait_ge(g["o_in_psum"], 2 * t + hf + 1)
                src = psum[:, (4 + hf) * BANK:(4 + hf) * BANK + 4 * VF_STRIDE].rearrange(
                    "p (h c) -> p h c", h=4)
                rec = k.o_rec[:, 4 * hf:4 * hf + 4]
                if t >= 1:
                    c.settle()
                c.did(V.reciprocal(rec, src[:, :, FD]))
                c.settle()
                if t >= 2 and hf == 0:
                    dve.wait_ge(g["ot_in_psum"], t - 1)
                dst = k.o[:, t % 2, hf * 4 * FD:(hf + 1) * 4 * FD].rearrange("p (h d) -> p h d", h=4)
                c.did(V.tensor_tensor(dst, src[:, :, 0:FD],
                                      widen(rec.rearrange("p (h o) -> p h o", o=1), [P, 4, FD]), ALU.mult),
                      g["o_normed"])

        def add_residual(n):
            dve.wait_ge(g["wo_in_psum"], n + 1)
            for half, shift in ((slice(0, 64), 0), (slice(64, P), 1)):
                x = k.xw[half, n * BANK + shift:(n + 1) * BANK + shift]
                c.did(V.tensor_tensor(x, x, psum[half, 7 * BANK:8 * BANK], ALU.add),
                      g["resid_done"] if shift else None)

        def row_stats(i):
            dve.wait_ge(g["xt_in_psum"], i + 1)
            for t in range(4):
                c.did(V.bn_stats(k.stats[:, 4 * i + t, :], psum[:, 7 * BANK + t * P:7 * BANK + (t + 1) * P]))
            c.settle()
            for t in range(4):
                c.did(V.bn_aggr(k.mv[:, 4 * i + t, :], k.stats[:, 4 * i + t, :]), g["mv_ready"] if t == 3 else None)

        def normalise_rows(i):
            dve.wait_ge(g["rstd_ready"], i + 1)
            for t in range(4):
                n = 4 * i + t
                c.did(V.tensor_scalar(k.xn[:, n, :], psum[:, 7 * BANK + t * P:7 * BANK + (t + 1) * P],
                                      k.mv[:, n, 0:1], k.rstd[:, n, :],
                                      ALU.subtract, ALU.mult), g["xn_ready"] if t == 3 else None)

        def gate(n):
            i, j = divmod(n, 3)
            rows = HID_BLOCKS[j][1]
            dve.wait_ge(g["gelu_ready"], n + 1)
            a = psum[0:rows, 2 * (n % 2) * BANK:(2 * (n % 2) + 1) * BANK]
            c.did(V.scalar_tensor_tensor(k.u[0:rows, i, j, :], a, k.b1[0:rows, j:j + 1],
                                         k.gelu[0:rows, n % 2, :], ALU.add, ALU.mult), g["u_ready"])

        def finish(n):
            dve.wait_ge(g["y_in_psum"], n + 1)
            for half, shift in ((slice(0, 64), 0), (slice(64, P), 1)):
                cols = slice(n * BANK + shift, (n + 1) * BANK + shift)
                c.did(V.scalar_tensor_tensor(keep.xs[half, b, cols], psum[half, Y_BANK[n] * BANK:(Y_BANK[n] + 1) * BANK],
                                             k.vec[half, 2:3], k.xw[half, cols], ALU.add, ALU.add))

        for t in range(TILES - 1):
            norm_out(t)
        add_residual(0)
        row_stats(0)
        norm_out(TILES - 1)
        normalise_rows(0)
        add_residual(1)
        gate(0)
        row_stats(1)
        gate(1)
        normalise_rows(1)
        gate(2)
        gate(3)
        finish(0)
        gate(4)
        gate(5)
        finish(1)
        c.settle()

    block.__exit__(None, None, None)
    k.clear_semaphores()


def ffn_half(nc, psum, dram, keep):
    with Scope(nc, "ffn") as k:
        sb = k.sb
        k.w_qkv, k.w_o = sb("w_qkv", [P, 3 * INNER]), sb("w_o", [P, INNER // P, D])
        k.w1, k.w2 = sb("w1", [P, 2 * HID]), sb("w2", [P, 3, D])
        k.vec, k.b1, k.qk_scale = sb("vec", [P, 3]), sb("b1", [P, 6]), sb("qk_scale", [P, 2 * FD])
        k.base_cos, k.base_sin, k.cos, k.sin = (sb(n, [P, TILES, 2 * FD])
                                                for n in ("base_cos", "base_sin", "cos", "sin"))
        k.xw = sb("xw", [P, S + 2])
        k.rot, k.rot_sin = sb("rot", [P, 2, 2 * INNER]), sb("rot_sin", [P, 2, 2 * INNER])
        k.sq = sb("sq", [P, 2 * INNER])
        k.ssq, k.root, k.rnorm, k.refine = (sb(n, [P, 2, 2 * FH]) for n in ("ssq", "root", "rnorm", "refine"))
        k.q_t, k.k_t = sb("q_t", [P, FH // 2, S]), sb("k_t", [P, FH, S])
        k.q_t_bf = k.q_t[:].bitcast(BF16).rearrange("p i (t w) -> p i t w", w=2)
        k.k_t_bf = k.k_t[:].bitcast(BF16).rearrange("p i (t w) -> p i t w", w=2)
        k.v = sb("v", [P, TILES, VF_COLS])
        k.band_bf, k.band_t_bf = sb("band", [P, SPAN_F], BF16), sb("band_t", [P, SPAN_F], BF16)
        k.pick = sb("pick", [P, FH, P], BF16)
        k.row_max, k.neg_max = sb("row_max", [P, TILES, FH]), sb("neg_max", [P, TILES, FH], BF16)
        k.max_t = sb("max_t", [P, S], BF16)
        k.probs = sb("probs", [P, 3, FH, SPAN_F])
        k.o, k.o_rec, k.o_t = sb("o", [P, 2, INNER]), sb("o_rec", [P, FH]), sb("o_t", [P, INNER // P, BANK])
        k.stats, k.mv, k.rstd = sb("stats", [P, TILES, 6]), sb("mv", [P, TILES, 2]), sb("rstd", [P, TILES, 1])
        k.xn = k.sq[:].rearrange("p (t d) -> p t d", t=TILES)
        k.hn = k.rot_sin[:, 0, :]
        k.gelu = k.rot_sin[:, 1, :].rearrange("p (i c) -> p i c", i=2)
        k.u = flat(k.q_t[:])[:, 0:6 * BANK].rearrange("p (c j t) -> p c j t", c=2, j=3)
        band, band_t, pick = k.u[:, 0, 0, 0:SPAN_F], k.u[:, 0, 1, 0:SPAN_F], flat(k.u[:, 1, 0:2, :])
        loaded, zeroed = k.sem("loaded"), k.sem("zeroed")
        k.layer_loaded, k.tables_done = k.sem("layer_loaded"), k.sem("tables_done")
        k.signals = {n: k.sem(n) for n in FFN_SIGNALS}
        with nc.Block() as block:
            @block.sync
            def _(sp):
                for dst, src in ((k.base_cos[:], dram["f_cos"]), (k.base_sin[:], dram["f_sin"]),
                                 (band, dram["f_band"]),
                                 (band_t, dram["f_band_t"]), (pick, dram["f_pick"])):
                    sp.dma_start(dst, src).then_inc(loaded, 16)

            @block.gpsimd
            def _(pool):
                pool.memset(k.k_t[:], 0.0)
                pool.memset(k.max_t[:], 0.0)
                pool.memset(k.v[:], 0.0).then_inc(zeroed, 1)
                pool.wait_ge(zeroed, 1)
                ones = k.v[:, :, 0:FH * VF_STRIDE].rearrange("p t (h c) -> p t h c", h=FH)[:, :, :, FD:FD + 1]
                pool.memset(ones, 1.0)

            @block.vector
            def _(dve):
                dve.wait_ge(loaded, 80)
                nc.vector.tensor_copy(k.band_bf[:], band)
                nc.vector.tensor_copy(k.band_t_bf[:], band_t)
                nc.vector.tensor_copy(flat(k.pick[:]), pick)
        k.clear_semaphores()
        with nc.Fori(0, DEPTH) as layer:
            load_layer(nc, dram, k, layer)
            with nc.Fori(0, B) as b:
                ffn_batch(nc, psum, keep, k, b)


def write_out(nc, psum, dram, keep):
    with Scope(nc, "out") as k:
        state, y = k.sb("state", [P, S]), k.sb("y", [P, TILES, D])
        state_ready, t_in_psum, y_ready, stored = (k.sem(n) for n in ("state", "t_in_psum", "y_ready", "stored"))
        gated = k.sem("gated")
        with nc.Fori(0, B) as b:
            with nc.Block() as block:
                @block.scalar
                def _(act):
                    for half, shift in ((slice(0, 64), 0), (slice(64, P), 1)):
                        act.activation(state[half, :], keep.xs[half, b, shift:shift + S],
                                       ACT.Copy).then_inc(state_ready, 1)

                @block.tensor
                def _(pe):
                    pe.wait_ge(state_ready, 2)
                    for t in range(TILES):
                        ins = nc.tensor.transpose(psum[:, t * P:(t + 1) * P], state[:, t * P:(t + 1) * P],
                                                  keep.ident[:])
                    ins.then_inc(t_in_psum, 1)

                @block.vector
                def _(dve):
                    dve.wait_ge(t_in_psum, 1)
                    nc.vector.tensor_tensor(
                        y[:], psum[:, 0:2 * BANK].rearrange("p (t d) -> p t d", t=TILES),
                        widen(keep.gate_b[:, b, :].rearrange("p (o d) -> p o d", o=1), [P, TILES, D]),
                        ALU.mult).then_inc(gated, 1)
                    dve.wait_ge(gated, 1)
                    nc.vector.tensor_tensor(y[:], y[:], keep.xres[:, b, :, :], ALU.add).then_inc(y_ready, 1)

                @block.sync
                def _(sp):
                    sp.wait_ge(y_ready, 1)
                    sp.dma_start(dram["out"][b].rearrange("(t p) d -> p t d", p=P), y[:]).then_inc(stored, 16)
                    sp.wait_ge(stored, 16)
            k.clear_semaphores()


def build_program(nc, dram):
    with ExitStack() as stack:
        psum = stack.enter_context(nc.psum_tensor("psum", [P, 8 * BANK], F32))
        keep = keep_tensors(nc, stack)
        prepare(nc, psum, dram, keep)
        attention_half(nc, psum, dram, keep)
        ffn_half(nc, psum, dram, keep)
        write_out(nc, psum, dram, keep)



def head_columns(w, heads):
    return w.reshape(D, heads, PAIRS, 2).transpose(0, 3, 2, 1).reshape(D, HEAD_DIM, heads)


def constants():
    f = np.float32
    pos = np.arange(S, dtype=f)
    rope_a = np.zeros((2, 2, S, HEAD_DIM), f)
    for a, base in enumerate(ROPE_BASES):
        inv = f(1) / np.power(f(base), np.arange(0, HEAD_DIM, 2, dtype=f) / f(HEAD_DIM))
        ang = (pos[:, None] * inv[None, :]).astype(f)
        cos, sin = np.cos(ang), np.sin(ang)
        rope_a[a, 0] = np.concatenate([cos, cos], 1)
        rope_a[a, 1] = np.concatenate([-sin, sin], 1)
    rope_a = rope_a.reshape(2, 2, TILES, P, HEAD_DIM).transpose(3, 0, 1, 2, 4)
    key, query = np.arange(P)[:, None], np.arange(SPAN_A)[None, :]
    local = ((query >= key) & (query - key < WINDOW_A)).astype(f)
    causal = (query[:, :P] >= key).astype(f)
    half = np.arange(0, FD, 2, dtype=f)
    ang = (pos[:, None] * (f(1) / np.power(f(10000), half / f(FD)))[None, :]).astype(f)
    base = (half + f(0.4 * FD)) / f(1.4 * FD)
    xpos = np.power(base[None, :], ((pos - S // 2) / f(WIN // 2))[:, None]).astype(f)
    cos, sin = np.cos(ang), np.sin(ang)
    both = lambda q, k_: np.concatenate([q, k_], 1).reshape(TILES, P, 2 * FD).transpose(1, 0, 2)
    twice = lambda lo, hi: np.concatenate([lo, hi], 1)
    f_cos = both(twice(cos * xpos, cos * xpos), twice(cos / xpos, cos / xpos))
    f_sin = both(twice(-sin * xpos, sin * xpos), twice(-sin / xpos, sin / xpos))
    q_pos, k_pos = np.arange(P)[:, None] + WIN, np.arange(SPAN_F)[None, :]
    seen = (k_pos <= q_pos) & (k_pos >= q_pos - WIN)
    k_pos, q_pos = np.arange(P)[:, None], np.arange(SPAN_F)[None, :]
    seen_t = (k_pos <= q_pos) & (k_pos >= q_pos - WIN)
    pick = np.zeros((P, FH, P), f)
    for head in range(FH):
        pick[head, head, :] = 1
    lower = np.arange(P) // 2 % 2
    return {
        "part": np.stack([1 - 2 * lower, lower], 1).astype(f),
        "f_cos": f_cos, "f_sin": f_sin, "f_band": np.where(seen, f(0), f(-1e30)),
        "f_band_t": np.where(seen_t, f(0), f(-1e30)),
        "f_pick": pick.reshape(P, FH * P),
        "identity": np.eye(P, dtype=f), "rope_a": rope_a, "local_mask": local[:, None, :],
        "causal_mask": causal[:, None, :],
        "eps": np.tile(np.array([[LN_EPS, ATT_EPS, 10 * np.log(2.0)]], f), (P, 1)),
    }


def layouts(x):
    a = lambda n: np.asarray(x[f"L0_attn_{n}"])
    q_k = np.concatenate([head_columns(a("l_wq"), HEADS), head_columns(a("l_wk"), KV_HEADS)], 2)
    g_q = head_columns(a("g_wq"), HEADS)
    up = head_columns(np.pad(a("g_k_up"), ((0, D - LATENT), (0, 0))), KV_HEADS)[:LATENT]
    out = {
        "hidden": a("hidden").reshape(B // PAIR, PAIR, TILES, P, D).transpose(0, 1, 3, 2, 4),
        "l_wqkv": np.concatenate([q_k.reshape(D, QK_COLS), a("l_wv")], 1),
        "g_wq": g_q, "kv_up": np.concatenate([up.reshape(LATENT, V_COLS), a("g_v_up")], 1),
        "kv_down_t": a("g_kv_down").T, "g_wo": a("g_wo"), "l_wo": a("l_wo"),
        "norm_w": np.stack([a("norm1_w"), a("norm2_w")], 1),
        "cond": np.asarray(x["L0_c"]).T, "wmod": np.asarray(x["L0_wmod"]),
    }
    w = lambda n: np.asarray(x[f"L0_ffn_{n}"])
    b1 = np.zeros((DEPTH, P, 6), np.float32)
    w2 = np.zeros((DEPTH, P, 3, D), np.float32)
    for j, (r0, rows) in enumerate(HID_BLOCKS):
        b1[:, :rows, j] = w("b1")[:, r0:r0 + rows]
        b1[:, :rows, 3 + j] = w("b1")[:, HID + r0:HID + r0 + rows]
        w2[:, :rows, j, :] = w("w2")[:, r0:r0 + rows, :]
    scale = np.concatenate([w("q_scale"), w("k_scale")], 1)
    out.update({
        "f_wqkv": w("wqkv"), "f_wo": w("wo").reshape(DEPTH, INNER // P, P, D).transpose(0, 2, 1, 3),
        "f_w1": w("w1"), "f_w2": w2, "f_b1": b1,
        "f_vec": np.stack([w("ln_g"), w("ln_b"), w("b2")], 2),
        "f_scale": np.broadcast_to(scale[:, None, :], (DEPTH, P, 2 * FD)),
    })
    return out


def kernel(**inputs):
    import concourse.bacc as bacc
    from concourse.bass_utils import run_bass_kernel_spmd

    nc = bacc.Bacc("TRN2", target_bir_lowering=False, num_devices=1)
    arrays, dram = {}, {}
    for name, value in {**layouts(inputs), **constants()}.items():
        value = np.ascontiguousarray(value)
        arrays[f"in_{name}"] = value
        dram[name] = nc.dram_tensor(f"in_{name}", value.shape, F32, kind="ExternalInput").ap()
    dram["out"] = nc.dram_tensor("out", (B, S, D), F32, kind="ExternalOutput").ap()
    build_program(nc, dram)
    result = run_bass_kernel_spmd(nc, [arrays], core_ids=[0])
    return result.results[0]["out"]
```
